# Optimizing a Trainium2 kernel written in Bass

```python
import numpy as np
import jax
import jax.numpy as jnp

def _softmax(x, axis=-1):
    return jax.nn.softmax(x, axis=axis)

def _gelu(x):
    return jax.nn.gelu(x, approximate=True)

def _silu(x):
    return jax.nn.silu(x)

def _sigmoid(x):
    return jax.nn.sigmoid(x)

def _layernorm(x, axis=-1, eps=1e-05):
    m = jnp.mean(x, axis=axis, keepdims=True)
    v = jnp.var(x, axis=axis, keepdims=True)
    return (x - m) / jnp.sqrt(v + eps)

def _scatter_add(tgt, idx, src, axis=0):
    return tgt.at[idx].add(src)

def _segment_sum(src, seg, n):
    return jax.ops.segment_sum(src, seg, n)
kernel_name = 'mk_gnn_ffn_d1_gnn_r8_321a0a'

def setup_inputs(seed: int=0):
    np.random.seed(seed)
    _w = jnp.asarray

    def _rec_inputs():
        import jax
        import jax.numpy as jnp
        _gk = jax.random.key(seed)
        x = -0.0002117 + 1 * jax.random.normal(jax.random.fold_in(_gk, 1), (6250, 512), jnp.float32)
        _s = jax.random.randint(jax.random.fold_in(_gk, 2), (50000,), 0, 6250, jnp.int32)
        _d = jax.random.randint(jax.random.fold_in(_gk, 3), (50000,), 0, 6250, jnp.int32)
        _loop = jnp.arange(6250, dtype=jnp.int32)
        src = jnp.concatenate([_s, _d, _loop])
        dst = jnp.concatenate([_d, _s, _loop])
        _o = jnp.argsort(dst, stable=True)
        src = src[_o]
        dst = dst[_o]
        return (x, src, dst)
    x, src, dst = _rec_inputs()

    def _L0_gnn_setup():
        import jax, jax.numpy as jnp
        import numpy as np
        N = 6250
        E = 50000
        D_IN = 512
        D_OUT = 512
        LN_EPS = 1e-05
        key = jax.random.key(seed)
        ks = jax.random.split(key, 8)
        x = jax.random.normal(ks[0], (N, D_IN), dtype=jnp.float32)
        src = jax.random.randint(ks[1], (E,), 0, N, dtype=jnp.int32)
        dst = jnp.sort(jax.random.randint(ks[2], (E,), 0, N, dtype=jnp.int32))
        bound = 1.0 / np.sqrt(D_IN)
        W_self = jax.random.uniform(ks[3], (D_IN, D_OUT), minval=-bound, maxval=bound, dtype=jnp.float32)
        b_self = jax.random.uniform(ks[4], (D_OUT,), minval=-bound, maxval=bound, dtype=jnp.float32)
        W_neigh = jax.random.uniform(ks[5], (D_IN, D_OUT), minval=-bound, maxval=bound, dtype=jnp.float32)
        gamma = jnp.ones((D_OUT,), dtype=jnp.float32)
        beta = jnp.zeros((D_OUT,), dtype=jnp.float32)
        alpha = jnp.array(0.25, dtype=jnp.float32)
        return {'x': x, 'src': src, 'dst': dst, 'W_self': W_self, 'b_self': b_self, 'W_neigh': W_neigh, 'gamma': gamma, 'beta': beta, 'alpha': alpha}
    _L0_gnn_all = _L0_gnn_setup()
    _L0_gnn_in = {k: v for k, v in _L0_gnn_all.items() if k in ('W_self', 'b_self', 'W_neigh', 'gamma', 'beta', 'alpha')}
    del _L0_gnn_all

    def _L0_ffn_setup():
        import jax, jax.numpy as jnp
        import numpy as np
        TOP_K = 2
        key = jax.random.key(seed)
        k1, k2, k3, k4 = jax.random.split(key, 4)
        B, S, D, F, E = (4, 512, 512, 256, 16)
        hidden_states = jax.random.normal(k1, (B, S, D), dtype=jnp.float32)
        gate_weight = jax.random.normal(k2, (E, D), dtype=jnp.float32) * 0.02
        w1 = jax.random.normal(k3, (E, F, D), dtype=jnp.float32) * 0.02
        w2 = jax.random.normal(k4, (E, D, F), dtype=jnp.float32) * 0.02
        return {'hidden_states': hidden_states, 'gate_weight': gate_weight, 'w1': w1, 'w2': w2}
    _L0_ffn_all = _L0_ffn_setup()
    _L0_ffn_in = {k: v for k, v in _L0_ffn_all.items() if k in ('gate_weight', 'w1', 'w2')}
    del _L0_ffn_all
    return {'x': x, 'src': src, 'dst': dst, 'L0_gnn_W_self': _L0_gnn_in['W_self'], 'L0_gnn_b_self': _L0_gnn_in['b_self'], 'L0_gnn_W_neigh': _L0_gnn_in['W_neigh'], 'L0_gnn_gamma': _L0_gnn_in['gamma'], 'L0_gnn_beta': _L0_gnn_in['beta'], 'L0_gnn_alpha': _L0_gnn_in['alpha'], 'L0_ffn_gate_weight': _L0_ffn_in['gate_weight'], 'L0_ffn_w1': _L0_ffn_in['w1'], 'L0_ffn_w2': _L0_ffn_in['w2']}

def reference(x, src, dst, L0_gnn_W_self, L0_gnn_b_self, L0_gnn_W_neigh, L0_gnn_gamma, L0_gnn_beta, L0_gnn_alpha, L0_ffn_gate_weight, L0_ffn_w1, L0_ffn_w2):
    import jax
    import jax.numpy as jnp

    def _L0_gnn_ref(x, src, dst, W_self, b_self, W_neigh, gamma, beta, alpha):
        import jax, jax.numpy as jnp
        import numpy as np
        N = 6250
        E = 50000
        D_IN = 512
        D_OUT = 512
        LN_EPS = 1e-05
        deg = jax.ops.segment_sum(jnp.ones_like(src, dtype=x.dtype), dst, num_segments=N)
        inv_deg = 1.0 / jnp.maximum(deg, 1.0)
        agg = jax.ops.segment_sum(x[src], dst, num_segments=N)
        neigh = agg * inv_deg[:, None]
        h = x @ W_self + b_self + neigh @ W_neigh
        mu = jnp.mean(h, axis=-1, keepdims=True)
        var = jnp.mean(jnp.square(h - mu), axis=-1, keepdims=True)
        h = (h - mu) * jax.lax.rsqrt(var + LN_EPS) * gamma + beta
        h = jnp.where(h >= 0, h, alpha * h)
        return h + x

    def _L0_ffn_ref(hidden_states, gate_weight, w1, w2):
        import jax, jax.numpy as jnp
        import numpy as np
        TOP_K = 2
        B, S, D = hidden_states.shape
        E = gate_weight.shape[0]
        x = hidden_states.reshape(-1, D)
        gate_logits = x @ gate_weight.T
        top_vals, top_idx = jax.lax.top_k(gate_logits, TOP_K)
        routing_w = jax.nn.softmax(top_vals, axis=-1)
        mask = jnp.any(top_idx[:, :, None] == jnp.arange(E)[None, None, :], axis=1)
        h = jax.nn.silu(jnp.einsum('td,efd->tef', x, w1))
        counts = jnp.sum(mask, axis=0)
        h_sum = jnp.einsum('tef,te->ef', h, mask.astype(h.dtype))
        h_mean = h_sum / jnp.maximum(counts, 1)[:, None].astype(h.dtype)
        y_mean = jnp.einsum('ef,edf->ed', h_mean, w2)
        y_mean = jnp.where((counts > 0)[:, None], y_mean, 0.0)
        out = jnp.einsum('tk,tkd->td', routing_w, y_mean[top_idx])
        return out.reshape(B, S, D)
    x = x + _L0_gnn_ref(_layernorm(x, axis=-1), src, dst, L0_gnn_W_self, L0_gnn_b_self, L0_gnn_W_neigh, L0_gnn_gamma, L0_gnn_beta, L0_gnn_alpha)
    x = x + _L0_ffn_ref(_layernorm(x, axis=-1)[None], L0_ffn_gate_weight, L0_ffn_w1, L0_ffn_w2)[0]
    return x

_drawn_inputs = setup_inputs


def setup_inputs(seed=0):
    import zlib

    import numpy as np

    out = dict(_drawn_inputs(seed))
    spreads = {'L0_gnn_gamma': (1.0, 0.2), 'L0_gnn_beta': (0.0, 0.1)}
    factors = {'L0_gnn_b_self': 3.914, 'L0_ffn_gate_weight': 8.0, 'L0_ffn_w1': 8.0, 'L0_ffn_w2': 8.0}
    for name, (base, spread) in spreads.items():
        noise = np.random.default_rng([zlib.crc32(name.encode()), seed]).standard_normal(out[name].shape)
        drawn = base * np.exp(spread * noise) if base else spread * noise
        out[name] = jnp.asarray(drawn.astype(out[name].dtype))
    for name, factor in factors.items():
        out[name] = (out[name] * factor).astype(out[name].dtype)
    return out
```

```python
import concourse.bass as bass
from concourse import mybir
from contextlib import ExitStack

P = 128
N, D, EXPERTS, FF = 6250, 512, 16, 256
EDGES = 106250
CHUNKS = D // P
TILES = -(-N // P)
TAIL = N - (TILES - 1) * P
UNROLL = 4
ROUNDS = (TILES - 1) // UNROLL
EDGE_TILES = -(-EDGES // P)
EDGE_CHUNKS = -(-EDGE_TILES // P)
STEPS = EDGE_TILES + TILES
HALF = 8
BODY = 2 * HALF
STEP_ROUNDS = STEPS // BODY
SLOTS = -(-2 * N // P) + EXPERTS
CAP = (TILES + 1) * P
DUMMY = EXPERTS * CAP
SCALE = 1024.0
EPS = 1e-5
CREDIT = 4
assert STEPS % BODY == 0 and TILES == UNROLL * ROUNDS + 1


def ready(i):
    return CREDIT + i + 1


def reuse(i, ring):
    return CREDIT - ring + i + 1


def masks(it, n):
    return UNROLL * it + n


class Count:

    def __init__(self, eng, sem, start):
        self.eng, self.sem, self.start, self.n = eng, sem, start, 0

    def link(self, ins):
        ins.then_inc(self.sem, 1)
        self.n += 1
        self.eng.wait_ge(self.sem, self.start + self.n)


def build(nc, x, src, dst, w_self, b_self, w_neigh, gamma, beta, alpha, gate_t, w1_t, w2_t, out):
    f32, f16, bf16, i32 = mybir.dt.float32, mybir.dt.float16, mybir.dt.bfloat16, mybir.dt.int32
    ALU = mybir.AluOpType
    ACT = mybir.ActivationFunctionType
    X = mybir.AxisListType.X
    ds = bass.ds

    ctx = ExitStack()
    with ctx:
        def sem(name):
            return ctx.enter_context(nc.semaphore(name))

        def sems(name, n):
            return [sem(f"{name}{i}") for i in range(n)]

        def sb(name, shape, dt=f32):
            return ctx.enter_context(nc.sbuf_tensor(name, shape, dt))

        table = nc.dram_tensor("table", [N, 2 * D], f16).ap()
        self_d = nc.dram_tensor("self_d", [TILES * P, D], f32).ap()
        resid_d = nc.dram_tensor("resid_d", [TILES * P, D], f32).ap()
        bucket = nc.dram_tensor("bucket", [DUMMY + P, D], f32).ap()

        agg = sb("agg", [P, TILES, D + 1])
        wn = sb("wn", [P, CHUNKS, D])
        gammab = sb("gammab", [P, D])
        betab = sb("betab", [P, D])
        alphab = sb("alphab", [P, 1])
        gwt = sb("gwt", [P, CHUNKS, EXPERTS])
        ident = sb("ident", [P, P])
        ones = sb("ones", [P, P])
        before = sb("before", [P, P])
        before16 = sb("before16", [P, P], bf16)
        ones16 = sb("ones16", [P, P], bf16)
        onesh = sb("onesh", [P, 1], f16)
        shift = sb("shift", [EXPERTS, EXPERTS + 1])
        iota_row = sb("iota_row", [P, P])
        iota_p = sb("iota_p", [P, EDGE_CHUNKS])
        pick = sb("pick", [P, EXPERTS])
        ecap = sb("ecap", [P, EXPERTS])
        rstd = sb("rstd", [P, TILES])
        nmr = sb("nmr", [P, TILES])
        inv = sb("inv", [P, TILES])
        first = sb("first", [P, TILES, EXPERTS])
        second = sb("second", [P, TILES, EXPERTS])
        top = sb("top", [P, 2, TILES])
        stats = sb("stats", [P, UNROLL, 6])
        mv = sb("mv", [P, UNROLL, 2])
        var = sb("var", [P, UNROLL])
        rec = sb("rec", [P, UNROLL])
        root = sb("root", [P, UNROLL])
        fix = sb("fix", [P, UNROLL])
        gs = sb("gs", [P, UNROLL])
        gb = sb("gb", [P, UNROLL])

        WORK = 18720
        work = sb("work", [P, WORK])
        place = [0]

        def cut(words, start=None):
            if start is not None:
                place[0] = start
            a = place[0]
            place[0] += words
            assert place[0] <= WORK, place[0]
            return work[:, a:a + words]

        xin = cut(UNROLL * D, 0).rearrange("p (b n) -> p b n", b=UNROLL)
        xs = cut(UNROLL * D).rearrange("p (b n) -> p b n", b=UNROLL)
        tb = cut(UNROLL * D).bitcast(f16).rearrange("p (b n) -> p b n", b=UNROLL)
        KW = STEPS + BODY
        a0 = place[0]
        idx_all = cut(KW).bitcast(i32)
        dstrel = cut(KW)
        jrow = cut(KW).bitcast(i32)
        b0 = place[0]
        srci = cut(EDGE_CHUNKS * P).bitcast(i32).rearrange("p (c e) -> p c e", c=EDGE_CHUNKS)
        dsti = cut(EDGE_CHUNKS * P).bitcast(i32).rearrange("p (c e) -> p c e", c=EDGE_CHUNKS)
        srcf = cut(EDGE_CHUNKS * P).rearrange("p (c e) -> p c e", c=EDGE_CHUNKS)
        dstf = cut(EDGE_CHUNKS * P).rearrange("p (c e) -> p c e", c=EDGE_CHUNKS)
        most = cut(EDGE_CHUNKS)
        bounds = cut(TILES - 1)
        passed = cut(EDGE_CHUNKS * (TILES - 1)).rearrange("p (c j) -> p c j", c=EDGE_CHUNKS)
        turn = cut(1)
        kvals = cut(STEPS)
        later = cut(STEPS)
        jall = cut(STEPS)
        tall = cut(STEPS)
        hit = cut(2 * STEPS).rearrange("p (a k) -> p a k", a=2)
        gath = cut(HALF * D, b0).bitcast(f16).rearrange("p (b n) -> p b n", b=HALF)
        hot = cut(BODY * P // 2).bitcast(f16).rearrange("p (h b n) -> p h b n", h=2, b=HALF)
        idxb = cut(BODY).bitcast(i32)
        ws = cut(CHUNKS * D, 0).rearrange("p (c n) -> p c n", c=CHUNKS)
        cx = cut(D)
        cxn = cut(D)
        cxt = cut(D).rearrange("p (c n) -> p c n", c=CHUNKS)
        cs = cut(D)
        cr = cut(D)
        bself = cut(D)
        assert place[0] <= a0
        scaled = cut(2 * D, 0).rearrange("p (b n) -> p b n", b=2)
        aggt = cut(2 * D).rearrange("p (b c n) -> p b c n", b=2, c=CHUNKS)
        sbuf = cut(2 * D).rearrange("p (b n) -> p b n", b=2)
        rbuf = cut(2 * D).rearrange("p (b n) -> p b n", b=2)
        x2 = cut(UNROLL * D).rearrange("p (b n) -> p b n", b=UNROLL)
        x2t = cut(2 * D).rearrange("p (b c n) -> p b c n", b=2, c=CHUNKS)
        neg = cut(D)
        GE = UNROLL * EXPERTS

        def small():
            return cut(GE).rearrange("p (b e) -> p b e", b=UNROLL)

        logit, cand, logit2, spot, prod = small(), small(), small(), small(), small()
        lead = cut(UNROLL)
        row = cut(2 * UNROLL).bitcast(i32)
        rowf = cut(2 * UNROLL)
        mask = cut(GE // 2).bitcast(bf16).rearrange("p (b e) -> p b e", b=UNROLL)
        run = cut((UNROLL + 1) * EXPERTS // 2).bitcast(bf16).rearrange("p (b e) -> p b e", b=UNROLL + 1)
        d_end = place[0]
        w1 = cut(CHUNKS * EXPERTS * FF, 0).rearrange("p (c n) -> p c n", c=CHUNKS)
        RING = 3
        xf = wn[:, 0:RING, :]
        xft = cut(RING * D).rearrange("p (b c n) -> p b c n", b=RING, c=CHUNKS)
        hid = cut(RING * FF).rearrange("p (b n) -> p b n", b=RING)
        hote = sb("hote", [P, SLOTS, EXPERTS], f16)
        hotk = sb("hotk", [P, RING, EXPERTS])
        rowk = sb("rowk", [1, SLOTS], i32)
        expk = sb("expk", [1, SLOTS], i32)
        fillrow = sb("fillrow", [1, EXPERTS], i32)
        es = sb("es", [P, 8])
        steps49 = sb("steps49", [EXPERTS, TILES])
        reach = sb("reach", [EXPERTS + 1, SLOTS])
        erow = sb("erow", [P, 4, SLOTS])
        zero = sb("zero", [P, D])
        w2 = w1[:, 0:2, :].rearrange("p a (r n) -> p (a r) n", n=2 * D)

        ps = ctx.enter_context(nc.psum_tensor("ps", [P, 8, 512], f32))

        s_const = sem("s_const")
        s_zero = sem("s_zero")
        s_w = sem("s_w")
        s_edge = sem("s_edge")
        s_pad = sem("s_pad")
        a_x, a_st = sems("a_x", UNROLL), sems("a_st", UNROLL)
        a_var, a_sqrt, a_stat, a_norm, a_lo = sem("a_var"), sem("a_sqrt"), sem("a_stat"), sem("a_norm"), sem("a_lo")
        b_cmp, b_cnt, b_later, b_jb, b_hit, b_acc, b_done = [sem(f"b_{n}") for n in
                                                             ("cmp", "cnt", "later", "jb", "hit", "acc", "done")]
        c_g = sems("c_g", HALF)
        c_step, c_sum, c_hot, c_idx = sem("c_step"), sem("c_sum"), sem("c_hot"), sem("c_idx")
        c_x, c_xn, c_r, c_t, c_xt, c_mm, c_s, c_rs, c_ss = [sem(f"c_{n}") for n in
                                                                  ("x", "xn", "r", "t", "xt", "mm", "s", "rs", "ss")]
        d_s, d_r = sems("d_s", 2), sems("d_r", 2)
        d_inv, d_sc, d_t, d_at, d_mm, d_h = [sem(f"d_{n}") for n in ("inv", "sc", "t", "at", "mm", "h")]
        d_var, d_sqrt, d_stat, d_hn, d_gm, d_x1 = [sem(f"d_{n}") for n in ("var", "sqrt", "stat", "hn", "gm", "x1")]
        d_var2, d_sqrt2, d_stat2, d_x2, d_t2, d_xt = [sem(f"d_{n}") for n in ("var2", "sqrt2", "stat2", "x2", "t2", "xt")]
        d_lg, d_mask, d_pos, d_row = [sem(f"d_{n}") for n in ("lg", "mask", "pos", "row")]
        d_sc1, d_sc2 = sems("d_sc1", UNROLL), sems("d_sc2", UNROLL)
        e_cnt, e_n, e_base, e_reach, e_list, e_done, e_fill, e_w1 = [sem(f"e_{n}") for n in
                                                                     ("cnt", "n", "base", "reach", "list", "done", "fill", "w1")]
        f_x = sems("f_x", RING)
        f_t, f_xt, f_mm, f_hid, f_hot, f_acc, f_end = [sem(f"f_{n}") for n in
                                                      ("t", "xt", "mm", "hid", "hot", "acc", "end")]
        g_w2, g_mean, g_tr, g_trs, g_diag, g_y, g_ys = [sem(f"g_{n}") for n in
                                                       ("w2", "mean", "tr", "trs", "diag", "y", "ys")]
        g_ex, g_exd, g_rw, g_rt, g_rts, g_o, g_x, g_out = [sem(f"g_{n}") for n in
                                                          ("ex", "exd", "rw", "rt", "rts", "o", "x", "out")]
        v_link = sem("v_link")
        p_link = sem("p_link")

        def rounds(eng, body):
            with eng.Fori(0, ROUNDS) as it:
                body(it, UNROLL, P)
            body(ROUNDS, 1, TAIL)

        block = ctx.enter_context(nc.Block())

        @block.sync
        def _(sp):
            sp.wait_ge(s_pad, 2)
            full = (EDGE_CHUNKS - 1) * P * P
            rows_left = (EDGES - full) // P
            rest = EDGES - full - rows_left * P
            for a, t in ((src, srci), (dst, dsti)):
                sp.dma_start(t[:, 0:EDGE_CHUNKS - 1, :],
                             a[0:full].rearrange("(c p e) -> p c e", p=P, e=P)).then_inc(s_edge, 16)
                sp.dma_start(t[0:rows_left, EDGE_CHUNKS - 1, :],
                             a[full:full + rows_left * P].rearrange("(p e) -> p e", e=P)).then_inc(s_edge, 16)
                sp.dma_start(t[rows_left:rows_left + 1, EDGE_CHUNKS - 1, 0:rest],
                             a[full + rows_left * P:EDGES].rearrange("(p e) -> p e", p=1)).then_inc(s_edge, 16)

            def load_x(it, n, rows):
                for b in range(n):
                    i = UNROLL * it + b
                    sp.wait_ge(a_norm, reuse(i, UNROLL))
                    sp.dma_start(xin[0:rows, b, :], x[ds(i * P, rows), :]).then_inc(a_x[b], 16)

            def store_table(it, n, rows):
                for b in range(n):
                    i = UNROLL * it + b
                    sp.wait_ge(a_lo, ready(i))
                    sp.dma_start(table[ds(i * P, rows), :], tb[0:rows, b, :]).then_inc(a_st[b], 16)

            load_x(0, UNROLL, P)
            sp.dma_start(gammab[:, :], gamma.to_broadcast([P, D])).then_inc(a_st[0], 16)
            sp.dma_start(betab[:, :], beta.to_broadcast([P, D])).then_inc(a_st[1], 16)
            sp.dma_start(alphab[:, :], alpha.to_broadcast([P, 1])).then_inc(a_st[2], 16)
            sp.dma_start(gwt[:, :, :], gate_t.rearrange("(c p) n -> p c n", p=P)).then_inc(a_st[3], 16)
            with sp.Fori(0, ROUNDS - 1) as it:
                load_x(it + 1, UNROLL, P)
                store_table(it, UNROLL, P)
            load_x(ROUNDS, 1, TAIL)
            store_table(ROUNDS - 1, UNROLL, P)
            store_table(ROUNDS, 1, TAIL)

            sp.dma_start(wn[:, :, :], w_neigh.rearrange("(c p) n -> p c n", p=P)).then_inc(s_w, 16)
            for b in range(UNROLL):
                sp.wait_ge(a_st[b], 16 * (1 + ROUNDS + (b == 0)))
            sp.dma_start(ws[:, :, :], w_self.rearrange("(c p) n -> p c n", p=P)).then_inc(c_ss, 16)
            sp.dma_start(bself[0:1, :], b_self).then_inc(c_rs, 16)

            def side(i, rows):
                sp.wait_ge(c_r, i + 1)
                sp.dma_start(cx[0:rows, :], x[ds(i * P, rows), :]).then_inc(c_x, 16)
                sp.wait_ge(c_r, i + 2)
                sp.dma_start(resid_d[ds(i * P, rows), :], cr[0:rows, :]).then_inc(c_rs, 16)
                sp.wait_ge(c_s, i + 2)
                sp.dma_start(self_d[ds(i * P, rows), :], cs[0:rows, :]).then_inc(c_ss, 16)

            with sp.Fori(0, TILES - 1) as i:
                side(i, P)
            side(TILES - 1, TAIL)

            sp.wait_ge(c_ss, 16 * (TILES + 1))
            sp.wait_ge(c_rs, 16 * (TILES + 1))
            sp.wait_ge(d_inv, 1)

            def load_d(it, n, rows):
                for b in range(n):
                    i = UNROLL * it + b
                    sp.wait_ge(d_h, reuse(i, 2))
                    sp.dma_start(sbuf[0:rows, b % 2, :], self_d[ds(i * P, rows), :]).then_inc(d_s[b % 2], 16)
                for b in range(n):
                    i = UNROLL * it + b
                    sp.wait_ge(d_x1, reuse(i, 2))
                    sp.dma_start(rbuf[0:rows, b % 2, :], resid_d[ds(i * P, rows), :]).then_inc(d_r[b % 2], 16)

            rounds(sp, load_d)

            sp.wait_ge(e_cnt, 1)
            for b in range(UNROLL):
                sp.wait_ge(d_sc1[b], 16 * (1 + ROUNDS + (b == 0)))
                sp.wait_ge(d_sc2[b], 16 * (1 + ROUNDS + (b == 0)))
            sp.dma_start(w1[:, :, :], w1_t.rearrange("(c p) n -> p c n", p=P)).then_inc(e_w1, 16)
            sp.wait_ge(e_n, 1)
            for e in range(EXPERTS):
                at = sp.value_load(fillrow[0:1, e:e + 1], min_val=e * CAP, max_val=e * CAP + N)
                sp.dma_start(bucket[ds(at, P), :], zero[:, :]).then_inc(e_fill, 16)
            sp.wait_ge(e_fill, 16 * EXPERTS)
            sp.wait_ge(e_done, 1)

            with sp.Fori(0, SLOTS // RING) as it:
                for b in range(RING):
                    k = RING * it + b
                    sp.wait_ge(f_t, k + 1)
                    at = sp.value_load(rowk[0:1, ds(k, 1)], min_val=0, max_val=DUMMY)
                    sp.dma_start(xf[:, b, :], bucket[ds(at, P), :]).then_inc(f_x[b], 16)

            sp.wait_ge(f_mm, SLOTS + RING)
            for e in range(EXPERTS):
                sp.dma_start(w2[:, e % 8, :] if e < 8 else w1[:, 2 + (e - 8) // 4, ((e - 8) % 4) * 1024:((e - 8) % 4 + 1) * 1024],
                             w2_t[e, :, :].rearrange("(c p) n -> p c n", p=P)).then_inc(g_w2, 16)

            def store_out(it, n, rows):
                for b in range(n):
                    i = UNROLL * it + b
                    sp.wait_ge(g_x, ready(i))
                    sp.dma_start(out[ds(i * P, rows), :], agg[0:rows, ds(i, 1), 0:D]).then_inc(g_out, 16)

            rounds(sp, store_out)
            sp.wait_ge(g_out, 16 * TILES)

        @block.gpsimd
        def _(pool):
            ln = Count(pool, p_link, 0)
            pool.memset(srci[:, EDGE_CHUNKS - 1, :], 0).then_inc(s_pad, 1)
            pool.memset(dsti[:, EDGE_CHUNKS - 1, :], -1).then_inc(s_pad, 1)
            pool.memset(ones[:, :], 1.0)
            pool.memset(ones16[:, :], 1.0)
            pool.memset(top[:, :, :], 0.0)
            ln.link(pool.memset(onesh[:, :], 1.0))
            pool.iota(iota_row[:, :], pattern=[[1, P]], base=0, channel_multiplier=0, allow_small_or_imprecise_dtypes=True)
            pool.iota(iota_p[:, :], pattern=[[P, EDGE_CHUNKS]], base=0, channel_multiplier=1, allow_small_or_imprecise_dtypes=True)
            pool.iota(bounds[:, :], pattern=[[P, TILES - 1]], base=P, channel_multiplier=0, allow_small_or_imprecise_dtypes=True)
            pool.iota(kvals[:, :], pattern=[[1, STEPS]], base=0, channel_multiplier=0, allow_small_or_imprecise_dtypes=True)
            pool.iota(pick[:, :], pattern=[[-1, EXPERTS]], base=EXPERTS, channel_multiplier=0, allow_small_or_imprecise_dtypes=True)
            pool.iota(ecap[:, :], pattern=[[CAP, EXPERTS]], base=0, channel_multiplier=0, allow_small_or_imprecise_dtypes=True)
            pool.iota(steps49[:, :], pattern=[[P, TILES]], base=0, channel_multiplier=0, allow_small_or_imprecise_dtypes=True)
            pool.affine_select(out=ident[:, :], in_=ones[:, :], compare_op=ALU.is_equal, fill=0.0, base=0,
                               pattern=[[-1, P]], channel_multiplier=1)
            pool.affine_select(out=before[:, :], in_=ones[:, :], compare_op=ALU.is_gt, fill=0.0, base=0,
                               pattern=[[1, P]], channel_multiplier=-1)
            pool.affine_select(out=before16[:, :], in_=ones16[:, :], compare_op=ALU.is_gt, fill=0.0, base=0,
                               pattern=[[1, P]], channel_multiplier=-1)
            pool.affine_select(out=shift[:, :], in_=ones[0:EXPERTS, 0:EXPERTS + 1], compare_op=ALU.is_equal, fill=0.0,
                               base=-1, pattern=[[1, EXPERTS + 1]], channel_multiplier=-1).then_inc(s_const, 1)
            pool.memset(zero[:, :], 0.0).then_inc(s_zero, 1)
            pool.memset(agg[:, :, :], 0.0).then_inc(s_zero, 1)
            pool.sem_inc(a_lo, CREDIT)
            pool.sem_inc(d_gm, CREDIT)

            def low(it, n, rows):
                for b in range(n):
                    i = UNROLL * it + b
                    pool.wait_ge(a_norm, ready(i))
                    pool.tensor_tensor(tb[0:rows, b, D:2 * D], xs[0:rows, b, :], tb[0:rows, b, 0:D],
                                       ALU.subtract).then_inc(a_lo, 1)

            rounds(pool, low)

            for b in range(UNROLL):
                pool.wait_ge(a_st[b], 16 * (1 + ROUNDS + (b == 0)))
            pool.wait_ge(b_done, 1)
            with pool.Fori(0, STEP_ROUNDS) as it:
                for s in range(BODY):
                    if s % HALF == 0:
                        pool.wait_ge(c_idx, 2 * it + s // HALF + 1)
                    pool.wait_ge(c_step, BODY * it + s + 1 + HALF)
                    pool.nop(nofuse=True)
                    pool.indirect_dma_start(
                        out=gath[:, s % HALF, :], out_offset=None, in_=table[:, :],
                        in_offset=bass.IndirectOffsetOnAxis(ap=idxb[:, s:s + 1], axis=0)).then_inc(c_g[s % HALF], 16)

            part = P // (2 * UNROLL)
            for n, done in enumerate(d_sc1 + d_sc2):
                pool.dma_start(bucket[DUMMY + n * part:DUMMY + (n + 1) * part, :],
                               zero[n * part:(n + 1) * part, :]).then_inc(done, 16)

            def route(it, n, rows):
                for b in range(n):
                    i = UNROLL * it + b
                    pool.wait_ge(d_hn, ready(i))
                    pool.nop(nofuse=True)
                    pool.tensor_tensor(agg[0:rows, ds(i, 1), 0:D], agg[0:rows, ds(i, 1), 0:D],
                                       gammab[0:rows, :].unsqueeze(1), ALU.mult).then_inc(d_gm, 1)
                pool.wait_ge(d_row, it + 1)
                pool.nop(nofuse=True)
                for b in range(n):
                    for k, done in ((0, d_sc1), (1, d_sc2)):
                        pool.indirect_dma_start(
                            out=bucket[:, :], in_=x2[0:rows, b, :], in_offset=None,
                            out_offset=bass.IndirectOffsetOnAxis(ap=row[0:rows, k * UNROLL + b:k * UNROLL + b + 1], axis=0),
                        ).then_inc(done[b], 16)

            rounds(pool, route)

        @block.scalar
        def _(act):
            act.sem_inc(a_norm, CREDIT)
            act.sem_inc(c_xt, 1)
            act.sem_inc(c_s, 1)
            for s in (d_sc, d_at, d_hn, d_x2, d_xt, g_rts):
                act.sem_inc(s, CREDIT)
            act.sem_inc(f_hid, RING)

            def norm(it, n, rows):
                act.wait_ge(a_var, it + 1)
                act.activation(root[0:rows, 0:n], rec[0:rows, 0:n], ACT.Sqrt).then_inc(a_sqrt, 1)
                act.wait_ge(a_stat, it + 1)
                for b in range(n):
                    i = UNROLL * it + b
                    act.wait_ge(a_x[b], 16 * (it + 1))
                    act.wait_ge(a_lo, reuse(i, UNROLL))
                    act.activation(xs[0:rows, b, :], xin[0:rows, b, :], ACT.Identity,
                                   bias=gb[0:rows, b:b + 1], scale=gs[0:rows, b:b + 1])
                    act.wait_ge(a_st[b], 16 * (it + 1))
                    act.activation(tb[0:rows, b, 0:D], xin[0:rows, b, :], ACT.Identity,
                                   bias=gb[0:rows, b:b + 1], scale=gs[0:rows, b:b + 1]).then_inc(a_norm, 1)

            rounds(act, norm)

            act.wait_ge(b_done, 1)

            def index_copy(it, h):
                q = 2 * it + h
                act.wait_ge(c_step, HALF * q + HALF)
                act.nop(nofuse=True)
                act.copy(idxb[:, h * HALF:(h + 1) * HALF], idx_all[:, ds(HALF * q, HALF)]).then_inc(c_idx, 1)

            def side(i, rows):
                act.wait_ge(c_x, 16 * (i + 1))
                act.wait_ge(c_t, i + 1)
                act.wait_ge(c_r, i + 1)
                act.nop(nofuse=True)
                act.activation(cxn[0:rows, :], cx[0:rows, :], ACT.Identity, bias=nmr[0:rows, ds(i, 1)],
                               scale=rstd[0:rows, ds(i, 1)]).then_inc(c_xn, 1)
                act.wait_ge(c_t, i + 2)
                act.wait_ge(c_mm, i + 1)
                act.copy(cxt[:, :, 0:rows], ps[:, 4, :].rearrange("p (c n) -> p c n", c=CHUNKS)[:, :, 0:rows]).then_inc(c_xt, 1)
                act.wait_ge(c_mm, i + 2)
                act.wait_ge(c_ss, 16 * (i + 1))
                act.copy(cs[0:rows, :], ps[0:rows, 5, :]).then_inc(c_s, 1)

            with act.Fori(0, TILES - 1) as it:
                index_copy(it, 0)
                index_copy(it, 1)
                side(it, P)
            index_copy(TILES - 1, 0)
            index_copy(TILES - 1, 1)
            side(TILES - 1, TAIL)
            with act.Fori(TILES, STEP_ROUNDS) as it:
                index_copy(it, 0)
                index_copy(it, 1)

            act.wait_ge(d_inv, 1)

            def dense(it, n, rows):
                def scale(b):
                    i = UNROLL * it + b
                    act.wait_ge(d_t, reuse(i, 2))
                    act.nop(nofuse=True)
                    act.activation(scaled[0:rows, b % 2, :].unsqueeze(1), agg[0:rows, ds(i, 1), 0:D], ACT.Copy,
                                   scale=inv[0:rows, ds(i, 1)]).then_inc(d_sc, 1)

                def move_agg(b):
                    i = UNROLL * it + b
                    act.wait_ge(d_t, ready(i))
                    act.wait_ge(d_mm, reuse(i, 2))
                    act.copy(aggt[:, b % 2, :, 0:rows],
                             ps[:, b % 2, :].rearrange("p (c n) -> p c n", c=CHUNKS)[:, :, 0:rows]).then_inc(d_at, 1)

                scale(0)
                for b in range(1, n):
                    scale(b)
                    move_agg(b - 1)
                move_agg(n - 1)
                act.wait_ge(d_var, it + 1)
                act.activation(root[0:rows, 0:n], rec[0:rows, 0:n], ACT.Sqrt).then_inc(d_sqrt, 1)
                act.wait_ge(d_stat, it + 1)
                act.nop(nofuse=True)
                for b in range(n):
                    i = UNROLL * it + b
                    act.activation(agg[0:rows, ds(i, 1), 0:D], agg[0:rows, ds(i, 1), 0:D], ACT.Identity,
                                   bias=gb[0:rows, b:b + 1], scale=gs[0:rows, b:b + 1]).then_inc(d_hn, 1)
                act.wait_ge(d_var2, it + 1)
                act.activation(root[0:rows, 0:n], rec[0:rows, 0:n], ACT.Sqrt).then_inc(d_sqrt2, 1)
                act.wait_ge(d_stat2, it + 1)

                def norm2(b):
                    i = UNROLL * it + b
                    act.wait_ge(d_sc1[b], 16 * (it + 1))
                    act.wait_ge(d_sc2[b], 16 * (it + 1))
                    act.nop(nofuse=True)
                    act.activation(x2[0:rows, b, :].unsqueeze(1), agg[0:rows, ds(i, 1), 0:D], ACT.Identity,
                                   bias=gb[0:rows, b:b + 1], scale=gs[0:rows, b:b + 1]).then_inc(d_x2, 1)

                def move_x2(b):
                    i = UNROLL * it + b
                    act.wait_ge(d_t2, ready(i))
                    act.wait_ge(d_lg, reuse(i, 2))
                    act.copy(x2t[:, b % 2, :, 0:rows],
                             ps[:, 4 + b % 2, :].rearrange("p (c n) -> p c n", c=CHUNKS)[:, :, 0:rows]).then_inc(d_xt, 1)

                norm2(0)
                for b in range(1, n):
                    norm2(b)
                    move_x2(b - 1)
                move_x2(n - 1)

            rounds(act, dense)

            act.wait_ge(g_ex, 1)
            act.activation(top[:, 1, :], top[:, 1, :], ACT.Exp).then_inc(g_exd, 1)

            with act.Fori(0, SLOTS // RING) as it:
                for b in range(RING):
                    k = RING * it + b
                    act.wait_ge(f_mm, RING + k + 1)
                    act.wait_ge(f_acc, k + 1)
                    act.activation(hid[:, b, :], ps[:, 3 + b, 0:FF], ACT.Silu).then_inc(f_hid, 1)

            act.wait_ge(g_tr, 1)
            act.copy(hid[:, 0, 0:2 * EXPERTS], ps[:, 7, 0:2 * EXPERTS]).then_inc(g_trs, 1)

            def mix(it, n, rows):
                for b in range(n):
                    i = UNROLL * it + b
                    act.wait_ge(g_rt, ready(i))
                    act.wait_ge(g_o, reuse(i, 2))
                    act.copy(xft[0:EXPERTS, b % 2, 0, 0:rows], ps[0:EXPERTS, 1 + b % 2, 0:rows]).then_inc(g_rts, 1)

            rounds(act, mix)

        @block.tensor
        def _(pe):
            for s in (d_t, d_mm, d_t2, d_lg, g_rt, g_o):
                pe.sem_inc(s, CREDIT)
            pe.sem_inc(c_step, BODY)
            pe.sem_inc(c_t, 1)
            pe.sem_inc(c_mm, 1)
            pe.sem_inc(f_mm, RING)
            pe.sem_inc(f_t, RING)
            pe.sem_inc(f_acc, RING)

            NJ = TILES - 1
            pe.wait_ge(s_const, 1)
            pe.wait_ge(b_cmp, 1)
            for c in range(EDGE_CHUNKS):
                last = pe.matmul(ps[0:NJ, 6, 0:1], passed[:, c, :], ones[:, 0:1], start=c == 0,
                                 stop=c == EDGE_CHUNKS - 1)
            last.then_inc(b_cnt, 1)
            pe.wait_ge(b_later, 1)
            H = STEPS // 2
            for h in range(2):
                last = pe.matmul(ps[:, h, 0:H], ones[0:NJ, :], later[0:NJ, h * H:(h + 1) * H], start=True, stop=True)
            last.then_inc(b_jb, 1)
            for c in range(EDGE_CHUNKS):
                pe.wait_ge(b_hit, c + 1)
                for t, bank in ((srcf, 2), (dstf, 4)):
                    for h in range(2):
                        last = pe.matmul(ps[:, bank + h, 0:H], t[:, c, :], hit[:, c % 2, h * H:(h + 1) * H],
                                         start=c == 0, stop=c == EDGE_CHUNKS - 1)
                last.then_inc(b_acc, 1)

            pe.wait_ge(c_ss, 16)
            pe.wait_ge(c_rs, 16)
            pe.wait_ge(b_done, 1)

            def step(it, s):
                k = BODY * it + s
                b, h = s % HALF, s // HALF
                r = 2 * (s % 2)
                if b == 0:
                    pe.wait_ge(c_hot, 2 * it + h + 1)
                pe.wait_ge(c_g[b], 16 * (2 * it + h + 1))
                pe.wait_ge(c_sum, k + 1)
                oh = hot[:, h, b, :]
                pe.matmul(ps[:, r, :], oh, gath[:, b, 0:D], start=True, stop=False)
                pe.matmul(ps[:, r, :], oh, gath[:, b, D:2 * D], start=False, stop=True)
                pe.matmul(ps[:, r + 1, 0:1], oh, onesh[:, :], start=True, stop=True).then_inc(c_step, 1)

            def side_turn(i, rows):
                pe.wait_ge(c_xn, i + 1)
                pe.wait_ge(c_xt, i + 1)
                for c in range(CHUNKS):
                    last = pe.transpose(ps[:, 4, c * P:c * P + rows], cxn[0:rows, c * P:(c + 1) * P], ident[0:rows, 0:rows])
                last.then_inc(c_t, 1)

            def side_project(i, rows):
                pe.wait_ge(c_xt, i + 2)
                pe.wait_ge(c_s, i + 1)
                for c in range(CHUNKS):
                    pe.matmul(ps[0:rows, 5, :], cxt[:, c, 0:rows], ws[:, c, :], start=c == 0, stop=False)
                pe.matmul(ps[0:rows, 5, :], ones[0:1, 0:rows], bself[0:1, :], start=False, stop=True).then_inc(c_mm, 1)

            def body(it, rows):
                for s in range(BODY):
                    step(it, s)
                    if rows and s == 5:
                        side_turn(it, rows)
                    if rows and s == 9:
                        side_project(it, rows)

            with pe.Fori(0, TILES - 1) as it:
                body(it, P)
            body(TILES - 1, TAIL)
            with pe.Fori(TILES, STEP_ROUNDS) as it:
                body(it, 0)

            pe.wait_ge(s_w, 16)
            pe.wait_ge(d_inv, 1)

            def dense(it, n, rows):
                def turn_agg(b):
                    i = UNROLL * it + b
                    pe.wait_ge(d_sc, ready(i))
                    pe.wait_ge(d_at, reuse(i, 2))
                    for c in range(CHUNKS):
                        last = pe.transpose(ps[:, b % 2, c * P:c * P + rows], scaled[0:rows, b % 2, c * P:(c + 1) * P],
                                            ident[0:rows, 0:rows])
                    last.then_inc(d_t, 1)

                def project(b):
                    i = UNROLL * it + b
                    pe.wait_ge(d_at, ready(i))
                    pe.wait_ge(d_h, reuse(i, 2))
                    for c in range(CHUNKS):
                        last = pe.matmul(ps[0:rows, 2 + b % 2, :], aggt[:, b % 2, c, 0:rows], wn[:, c, :],
                                         start=c == 0, stop=c == CHUNKS - 1)
                    last.then_inc(d_mm, 1)

                def turn_x2(b):
                    i = UNROLL * it + b
                    pe.wait_ge(d_x2, ready(i))
                    pe.wait_ge(d_xt, reuse(i, 2))
                    for c in range(CHUNKS):
                        last = pe.transpose(ps[:, 4 + b % 2, c * P:c * P + rows], x2[0:rows, b, c * P:(c + 1) * P],
                                            ident[0:rows, 0:rows])
                    last.then_inc(d_t2, 1)

                def gate(b):
                    i = UNROLL * it + b
                    pe.wait_ge(d_xt, ready(i))
                    for c in range(CHUNKS):
                        last = pe.matmul(ps[0:rows, 6, b * EXPERTS:(b + 1) * EXPERTS], x2t[:, b % 2, c, 0:rows],
                                         gwt[:, c, :], start=c == 0, stop=c == CHUNKS - 1)
                    last.then_inc(d_lg, 1)

                for one, two in ((turn_agg, project), (turn_x2, gate)):
                    one(0)
                    for b in range(1, n):
                        one(b)
                        two(b - 1)
                    two(n - 1)
                pe.wait_ge(d_mask, masks(it, n))
                flat = lambda a: a[0:rows, 0:n, :].rearrange("p b e -> p (b e)")
                pe.matmul(ps[0:rows, 7, 0:n * EXPERTS], before16[0:rows, 0:rows], flat(mask), start=True, stop=False)
                pe.matmul(ps[0:rows, 7, 0:n * EXPERTS], ones16[:, 0:rows], run[:, 0:n, :].rearrange("p b e -> p (b e)"),
                          start=False, stop=True).then_inc(d_pos, 1)

            rounds(pe, dense)

            pe.wait_ge(d_row, ROUNDS + 1)
            pe.matmul(ps[0:EXPERTS, 6, 0:1], run[:, 0, :], ones16[:, 0:1], start=True, stop=True)
            pe.matmul(ps[0:1, 7, 0:EXPERTS], ones16[:, 0:1], run[:, 0, :], start=True, stop=True).then_inc(e_cnt, 1)
            pe.wait_ge(e_n, 1)
            pe.matmul(ps[0:EXPERTS + 1, 6, 1:2], before[0:EXPERTS, 0:EXPERTS + 1], es[0:EXPERTS, 1:2], start=True, stop=True)
            pe.matmul(ps[0:EXPERTS + 1, 7, 0:1], shift[:, :], es[0:EXPERTS, 1:2], start=True, stop=True).then_inc(e_base, 1)
            pe.wait_ge(e_reach, 1)
            pe.matmul(ps[:, 0, 0:SLOTS], ones[0:EXPERTS + 1, :], reach[:, :], start=True, stop=True)
            pe.matmul(ps[0:1, 1, 0:SLOTS], es[0:EXPERTS + 1, 3:4], reach[:, :], start=True, stop=True).then_inc(e_list, 1)

            pe.wait_ge(e_w1, 16)
            pe.wait_ge(e_done, 1)

            def turn(it, b):
                k = RING * it + b
                pe.wait_ge(f_x[b], 16 * (it + 1))
                pe.wait_ge(f_xt, k + 1)
                for c in range(CHUNKS):
                    last = pe.transpose(ps[:, b, c * P:(c + 1) * P], xf[:, b, c * P:(c + 1) * P], ident[:, :])
                last.then_inc(f_t, 1)

            def hidden(it, b):
                k = RING * it + b
                e = pe.value_load(expk[0:1, ds(k, 1)], min_val=0, max_val=EXPERTS - 1)
                pe.wait_ge(f_xt, RING + k + 1)
                pe.wait_ge(f_hid, k + 1)
                for c in range(CHUNKS):
                    last = pe.matmul(ps[:, 3 + b, 0:FF], xft[:, b, c, :], w1[:, c, ds(e * FF, FF)],
                                     start=c == 0, stop=c == CHUNKS - 1)
                last.then_inc(f_mm, 1)

            def collect(it, b):
                k = RING * it + b
                pe.wait_ge(f_hid, RING + k + 1)
                pe.wait_ge(f_hot, k + 1)
                pe.matmul(ps[0:EXPERTS, 6, 0:FF], hotk[:, b, :], hid[:, b, :], start=False, stop=False,
                          skip_group_check=True).then_inc(f_acc, 1)

            pe.matmul(ps[0:EXPERTS, 6, 0:FF], zero[:, 0:EXPERTS], zero[:, 0:FF], start=True, stop=False, skip_group_check=True)
            with pe.Fori(0, SLOTS // RING) as it:
                for b in range(RING):
                    turn(it, b)
                    if b:
                        hidden(it, b - 1)
                    if b > 1:
                        collect(it, b - 2)
                hidden(it, RING - 1)
                collect(it, RING - 2)
                collect(it, RING - 1)
            pe.matmul(ps[0:EXPERTS, 6, 0:FF], zero[:, 0:EXPERTS], zero[:, 0:FF], start=False, stop=True,
                      skip_group_check=True).then_inc(f_end, 1)

            pe.wait_ge(g_mean, 1)
            for c in range(FF // P):
                last = pe.transpose(ps[:, 7, c * EXPERTS:(c + 1) * EXPERTS], xf[0:EXPERTS, 0, c * P:(c + 1) * P],
                                    ident[0:EXPERTS, 0:EXPERTS])
            last.then_inc(g_tr, 1)
            pe.wait_ge(g_diag, 1)
            pe.wait_ge(g_w2, 16 * EXPERTS)
            for e in range(EXPERTS):
                for c in range(FF // P):
                    at = w2[:, e, c * D:(c + 1) * D] if e < 8 else \
                        w1[:, 2 + (e - 8) // 4, ((e - 8) % 4) * 1024 + c * D:((e - 8) % 4) * 1024 + (c + 1) * D]
                    last = pe.matmul(ps[0:EXPERTS, 0, :], xf[:, 1, (c * EXPERTS + e) * EXPERTS:(c * EXPERTS + e + 1) * EXPERTS],
                                     at, start=e == 0 and c == 0, stop=e == EXPERTS - 1 and c == FF // P - 1)
            last.then_inc(g_y, 1)
            pe.wait_ge(g_ys, 1)

            def mix(it, n, rows):
                def turn_weights(b):
                    i = UNROLL * it + b
                    pe.wait_ge(g_rw, ready(i))
                    pe.wait_ge(g_rts, reuse(i, 2))
                    pe.transpose(ps[0:EXPERTS, 1 + b % 2, 0:rows], hotk[0:rows, b % 2, :], ident[0:rows, 0:rows]).then_inc(g_rt, 1)

                def combine(b):
                    i = UNROLL * it + b
                    pe.wait_ge(g_rts, ready(i))
                    pe.wait_ge(g_x, reuse(i, 2))
                    pe.matmul(ps[0:rows, 3 + b % 2, :], xft[0:EXPERTS, b % 2, 0, 0:rows], xf[0:EXPERTS, 2, :],
                              start=True, stop=True).then_inc(g_o, 1)

                for b in range(n):
                    turn_weights(b)
                    combine(b)

            rounds(pe, mix)

        @block.vector
        def _(dve):
            for s in (d_h, d_x1, g_rw, g_x):
                dve.sem_inc(s, CREDIT)
            dve.sem_inc(c_sum, 2)
            dve.sem_inc(c_r, 1)
            dve.sem_inc(f_xt, RING)
            ln = Count(dve, v_link, 0)
            dve.wait_ge(s_edge, 16 * 6)
            dve.tensor_copy(dstf[:, :, :], dsti[:, :, :])
            ln.link(dve.tensor_copy(srcf[:, :, :], srci[:, :, :]))
            ln.link(dve.tensor_reduce(most[:, :], dstf[:, :, :], X, ALU.max))
            dve.wait_ge(s_const, 1)
            ln.link(dve.tensor_scalar(turn[:, :], iota_p[:, EDGE_CHUNKS - 1:EDGE_CHUNKS], float(EDGE_TILES), 1e6,
                                      ALU.is_ge, ALU.mult))
            ln.link(dve.tensor_tensor(most[:, EDGE_CHUNKS - 1:EDGE_CHUNKS], most[:, EDGE_CHUNKS - 1:EDGE_CHUNKS],
                                      turn[:, :], ALU.add))
            NJ = TILES - 1
            dve.tensor_tensor(passed[:, :, :], bounds[:, :].unsqueeze(1).to_broadcast([P, EDGE_CHUNKS, NJ]),
                              most[:, :].unsqueeze(2).to_broadcast([P, EDGE_CHUNKS, NJ]), ALU.is_gt).then_inc(b_cmp, 1)
            dve.wait_ge(b_cnt, 1)
            ln.link(dve.tensor_tensor(turn[0:NJ, :], ps[0:NJ, 6, 0:1], iota_p[0:NJ, 0:1], ALU.add))
            dve.tensor_scalar(later[0:NJ, :], kvals[0:NJ, :], turn[0:NJ, :], None, ALU.is_gt).then_inc(b_later, 1)
            dve.wait_ge(b_jb, 1)
            H = STEPS // 2
            jsplit = jall[:, :].rearrange("p (h k) -> p h k", h=2)
            ln.link(dve.tensor_copy(jsplit, ps[:, 0:2, 0:H]))
            dve.tensor_copy(jrow[0:1, 0:STEPS], jall[0:1, :])
            ln.link(dve.tensor_tensor(tall[:, :], kvals[:, :], jall[:, :], ALU.subtract))
            for c in range(EDGE_CHUNKS):
                if c >= 2:
                    dve.wait_ge(b_acc, c - 1)
                dve.tensor_scalar(hit[:, c % 2, :], tall[:, :], iota_p[:, c:c + 1], None, ALU.is_equal).then_inc(b_hit, 1)
            dve.wait_ge(b_acc, EDGE_CHUNKS)
            dve.memset(dstrel[:, STEPS:KW], 0.0)
            dve.tensor_copy(idx_all[:, 0:STEPS].rearrange("p (h k) -> p h k", h=2), ps[:, 2:4, 0:H])
            dve.scalar_tensor_tensor(dstrel[:, 0:STEPS].rearrange("p (h k) -> p h k", h=2), jsplit, -float(P),
                                     ps[:, 4:6, 0:H], ALU.mult, ALU.add).then_inc(b_done, 1)
            count = ln.n

            def rstd_chain(ln, n, rows, mean_var, var_sem, sqrt_sem, turns):
                r = slice(0, rows)
                m = slice(0, n)
                ln.link(dve.tensor_scalar(var[r, m], mean_var[r, m, 1], EPS, None, ALU.add))
                dve.reciprocal(rec[r, m], var[r, m]).then_inc(var_sem, 1)
                dve.wait_ge(sqrt_sem, turns)
                ln.link(dve.tensor_tensor(fix[r, m], root[r, m], root[r, m], ALU.mult))
                ln.link(dve.tensor_tensor(fix[r, m], fix[r, m], var[r, m], ALU.mult))
                ln.link(dve.tensor_scalar(fix[r, m], fix[r, m], -0.5, 1.5, ALU.mult, ALU.add))

            def aggregate(ln, last, n, r):
                ln.link(last)
                dve.nop(nofuse=True)
                for b in range(n):
                    last = dve.bn_aggr(mv[r, b, :], stats[r, b, :])
                ln.link(last)

            A_LINKS = 8

            def norm_a(it, n, rows):
                ln = Count(dve, v_link, count + it * A_LINKS)
                r = slice(0, rows)
                for b in range(n):
                    dve.wait_ge(a_x[b], 16 * (it + 1))
                    last = dve.bn_stats(stats[r, b, :], xin[r, b, :])
                aggregate(ln, last, n, r)
                rstd_chain(ln, n, rows, mv, a_var, a_sqrt, it + 1)
                at = ds(it * UNROLL, n)
                ln.link(dve.tensor_tensor(rstd[r, at], root[r, 0:n], fix[r, 0:n], ALU.mult))
                ln.link(dve.scalar_tensor_tensor(nmr[r, at], mv[r, 0:n, 0], -1.0, rstd[r, at], ALU.mult, ALU.mult))
                dve.wait_ge(a_norm, CREDIT + UNROLL * it)
                dve.tensor_scalar(gs[r, 0:n], rstd[r, at], SCALE, None, ALU.mult)
                dve.tensor_scalar(gb[r, 0:n], nmr[r, at], SCALE, None, ALU.mult).then_inc(a_stat, 1)
                assert ln.n == A_LINKS, ln.n

            rounds(dve, norm_a)
            count += A_LINKS * ROUNDS + A_LINKS

            dve.wait_ge(s_zero, 2)

            def one_hots(q, h):
                dve.wait_ge(c_step, HALF * q + HALF)
                dve.tensor_tensor(hot[:, h, :, :], iota_row[:, :].unsqueeze(1).to_broadcast([P, HALF, P]),
                                  dstrel[:, ds(HALF * q, HALF)].unsqueeze(2).to_broadcast([P, HALF, P]),
                                  ALU.is_equal).then_inc(c_hot, 1)

            def add_step(it, s):
                k = BODY * it + s
                j = dve.value_load(jrow[0:1, ds(k, 1)], min_val=0, max_val=TILES - 1)
                dve.wait_ge(c_step, BODY + k + 1)
                dve.wait_ge(c_sum, 2 + k)
                r = 2 * (s % 2)
                dve.tensor_tensor(agg[:, ds(j, 1), :], agg[:, ds(j, 1), :],
                                  ps[:, r:r + 2, :].rearrange("p a n -> p (a n)")[:, 0:D + 1].unsqueeze(1),
                                  ALU.add).then_inc(c_sum, 1)

            def side(i, rows):
                dve.wait_ge(c_xn, i + 1)
                dve.wait_ge(c_rs, 16 * (i + 1))
                dve.tensor_tensor(cr[0:rows, :], cx[0:rows, :], cxn[0:rows, :], ALU.add).then_inc(c_r, 1)

            def body(it, rows):
                one_hots(2 * it + 1, 1)
                for s in range(BODY):
                    add_step(it, s)
                    if s == HALF - 1:
                        one_hots(2 * it + 2, 0)
                    if rows and s == 4:
                        side(it, rows)

            one_hots(0, 0)
            with dve.Fori(0, TILES - 1) as it:
                body(it, P)
            body(TILES - 1, TAIL)
            with dve.Fori(TILES, STEP_ROUNDS) as it:
                body(it, 0)

            dve.wait_ge(c_sum, 2 + STEPS)
            dve.wait_ge(c_ss, 16 * (TILES + 1))
            dve.wait_ge(c_rs, 16 * (TILES + 1))
            ln = Count(dve, v_link, count)
            ln.link(dve.memset(run[:, 0, :], 0.0))
            ln.link(dve.tensor_scalar(inv[:, :], agg[:, :, D], 1.0, None, ALU.max))
            ln.link(dve.reciprocal(inv[:, :], inv[:, :]))
            dve.tensor_scalar(inv[:, :], inv[:, :], 1.0 / SCALE, None, ALU.mult).then_inc(d_inv, 1)
            dve.wait_ge(s_w, 16)
            count += ln.n
            D_LINKS = {n: 3 * n + 32 for n in (UNROLL, 1)}

            def dense(it, n, rows):
                ln = Count(dve, v_link, count + it * D_LINKS[UNROLL])
                r, m = slice(0, rows), slice(0, n)
                for b in range(n):
                    i = UNROLL * it + b
                    slot = agg[r, ds(i, 1), 0:D]
                    dve.wait_ge(d_mm, ready(i))
                    dve.wait_ge(d_s[b % 2], 16 * (2 * it + b // 2 + 1) if n > 1 else 16 * (2 * ROUNDS + 1))
                    dve.tensor_tensor(slot, ps[r, 2 + b % 2, :].unsqueeze(1), sbuf[r, b % 2, :].unsqueeze(1), ALU.add).then_inc(d_h, 1)
                    dve.wait_ge(d_h, ready(i))
                    dve.nop(nofuse=True)
                    last = dve.bn_stats(stats[r, b, :], slot)
                aggregate(ln, last, n, r)
                rstd_chain(ln, n, rows, mv, d_var, d_sqrt, it + 1)
                ln.link(dve.tensor_tensor(gs[r, m], root[r, m], fix[r, m], ALU.mult))
                dve.scalar_tensor_tensor(gb[r, m], mv[r, m, 0], -1.0, gs[r, m], ALU.mult, ALU.mult).then_inc(d_stat, 1)
                for b in range(n):
                    i = UNROLL * it + b
                    slot = agg[r, ds(i, 1), 0:D]
                    low = neg[r, :].unsqueeze(1)
                    dve.wait_ge(d_gm, ready(i))
                    ln.link(dve.tensor_tensor(slot, slot, betab[r, :].unsqueeze(1), ALU.add))
                    ln.link(dve.tensor_scalar(low, slot, 0.0, alphab[r, :], ALU.min, ALU.mult))
                    ln.link(dve.scalar_tensor_tensor(slot, slot, 0.0, low, ALU.max, ALU.add))
                    dve.wait_ge(d_r[b % 2], 16 * (2 * it + b // 2 + 1) if n > 1 else 16 * (2 * ROUNDS + 1))
                    dve.tensor_tensor(slot, slot, rbuf[r, b % 2, :].unsqueeze(1), ALU.add).then_inc(d_x1, 1)
                    dve.wait_ge(d_x1, ready(i))
                    dve.nop(nofuse=True)
                    last = dve.bn_stats(stats[r, b, :], slot)
                aggregate(ln, last, n, r)
                rstd_chain(ln, n, rows, mv, d_var2, d_sqrt2, it + 1)
                ln.link(dve.tensor_tensor(gs[r, m], root[r, m], fix[r, m], ALU.mult))
                dve.scalar_tensor_tensor(gb[r, m], mv[r, m, 0], -1.0, gs[r, m], ALU.mult, ALU.mult).then_inc(d_stat2, 1)

                dve.wait_ge(d_lg, CREDIT + UNROLL * it + n)
                at = ds(it * UNROLL, n)
                wide = lambda a: a.unsqueeze(2).to_broadcast([rows, n, EXPERTS])
                over = lambda a: a[r, :].unsqueeze(1).to_broadcast([rows, n, EXPERTS])
                ln.link(dve.tensor_copy(logit[r, m, :], ps[r, 6, 0:n * EXPERTS].rearrange("p (b e) -> p b e", b=n)))
                for k, (vals, pickd) in enumerate(((logit, first), (logit2, second))):
                    best = top[r, k, at]
                    ln.link(dve.tensor_reduce(best, vals[r, m, :], X, ALU.max))
                    ln.link(dve.tensor_tensor(cand[r, m, :], vals[r, m, :], wide(best), ALU.is_equal))
                    ln.link(dve.tensor_tensor(cand[r, m, :], cand[r, m, :], over(pick), ALU.mult))
                    ln.link(dve.tensor_reduce(lead[r, m], cand[r, m, :], X, ALU.max))
                    ln.link(dve.tensor_tensor(pickd[r, at, :], cand[r, m, :], wide(lead[r, m]), ALU.is_equal))
                    if k == 0:
                        ln.link(dve.scalar_tensor_tensor(logit2[r, m, :], first[r, at, :], -3.0e38, logit[r, m, :],
                                                         ALU.mult, ALU.add))
                both_picks = dve.tensor_tensor(mask[r, m, :], first[r, at, :], second[r, at, :], ALU.add)
                for b in range(n - 1):
                    both_picks.then_inc(d_mask, 1)
                    dve.wait_ge(d_mask, masks(it, b + 1))
                    both_picks = dve.tensor_tensor(run[r, b + 1, :], run[r, b, :], mask[r, b, :], ALU.add)
                both_picks.then_inc(d_mask, 1)
                dve.wait_ge(d_mask, masks(it, n))
                dve.wait_ge(d_pos, it + 1)
                ln.link(dve.tensor_tensor(spot[r, m, :], ps[r, 7, 0:n * EXPERTS].rearrange("p (b e) -> p b e", b=n),
                                          over(ecap), ALU.add))
                ln.link(dve.tensor_tensor(run[r, 0, :], run[r, n - 1, :], mask[r, n - 1, :], ALU.add))
                for k, pickd in enumerate((first, second)):
                    ln.link(dve.tensor_tensor(prod[r, m, :], pickd[r, at, :], spot[r, m, :], ALU.mult))
                    ln.link(dve.tensor_reduce(rowf[r, k * UNROLL:k * UNROLL + n], prod[r, m, :], X, ALU.add))
                for b in range(UNROLL if n > 1 else UNROLL):
                    dve.wait_ge(d_sc1[b], 16 * (it + 1))
                    dve.wait_ge(d_sc2[b], 16 * (it + 1))
                both = lambda a: a[r, :].rearrange("p (k b) -> p k b", k=2)[:, :, 0:n]
                dve.tensor_copy(both(row), both(rowf)).then_inc(d_row, 1)
                assert ln.n == D_LINKS[n], (n, ln.n)

            rounds(dve, dense)
            count += D_LINKS[UNROLL] * ROUNDS + D_LINKS[1]

            ln = Count(dve, v_link, count)
            E1 = EXPERTS + 1
            dve.wait_ge(e_cnt, 1)
            ln.link(dve.tensor_copy(es[0:EXPERTS, 0:1], ps[0:EXPERTS, 6, 0:1]))
            ln.link(dve.tensor_tensor(fillrow[0:1, :], ps[0:1, 7, 0:EXPERTS], ecap[0:1, :], ALU.add))
            ln.link(dve.tensor_scalar(steps49[:, :], steps49[:, :], es[0:EXPERTS, 0:1], None, ALU.is_lt))
            dve.tensor_reduce(es[0:EXPERTS, 1:2], steps49[:, :], X, ALU.add).then_inc(e_n, 1)
            ln.link(dve.tensor_scalar(es[0:EXPERTS, 4:5], es[0:EXPERTS, 0:1], 1.0, None, ALU.max))
            ln.link(dve.reciprocal(es[0:EXPERTS, 5:6], es[0:EXPERTS, 4:5]))
            dve.wait_ge(e_base, 1)
            ln.link(dve.tensor_copy(es[0:E1, 2:3], ps[0:E1, 6, 1:2]))
            ln.link(dve.tensor_scalar(es[0:E1, 3:4], ps[0:E1, 7, 0:1], -float(P), float(CAP), ALU.mult, ALU.add))
            dve.tensor_scalar(reach[:, :], iota_row[0:E1, 0:SLOTS], es[0:E1, 2:3], None, ALU.is_ge).then_inc(e_reach, 1)
            dve.wait_ge(e_list, 1)
            past = erow[:, 0, :]
            ln.link(dve.tensor_copy(past, ps[:, 0, 0:SLOTS]))
            dve.tensor_tensor(hote[:, :, :], past.unsqueeze(2).to_broadcast([P, SLOTS, EXPERTS]),
                              pickup(dve, iota_row, P, SLOTS, EXPERTS), ALU.is_equal)
            ln.link(dve.tensor_scalar(expk[0:1, :], past[0:1, :], float(EXPERTS), -1.0, ALU.min, ALU.add))
            one, two, three = erow[0:1, 1, :], erow[0:1, 2, :], erow[0:1, 3, :]
            ln.link(dve.scalar_tensor_tensor(one, iota_row[0:1, 0:SLOTS], float(P), ps[0:1, 1, 0:SLOTS], ALU.mult, ALU.add))
            ln.link(dve.tensor_scalar(one, one, -float(CAP), None, ALU.add))
            ln.link(dve.tensor_scalar(two, past[0:1, :], float(EXPERTS), None, ALU.is_gt))
            ln.link(dve.tensor_scalar(three, two, -1.0, 1.0, ALU.mult, ALU.add))
            ln.link(dve.tensor_tensor(one, one, three, ALU.mult))
            ln.link(dve.scalar_tensor_tensor(rowk[0:1, :], two, float(DUMMY), one, ALU.mult, ALU.add))
            dve.tensor_tensor(top[:, 1, :], top[:, 1, :], top[:, 0, :], ALU.subtract).then_inc(g_ex, 1)
            dve.wait_ge(g_exd, 1)
            ln.link(dve.tensor_scalar(top[:, 0, :], top[:, 1, :], 1.0, None, ALU.add))
            ln.link(dve.reciprocal(top[:, 0, :], top[:, 0, :]))
            dve.tensor_tensor(top[:, 1, :], top[:, 1, :], top[:, 0, :], ALU.mult).then_inc(e_done, 1)
            count += ln.n

            with dve.Fori(0, SLOTS // RING) as it:
                for b in range(RING):
                    k = RING * it + b
                    dve.wait_ge(f_acc, k + 1)
                    dve.tensor_copy(hotk[:, b:b + 1, :], hote[:, ds(k, 1), :]).then_inc(f_hot, 1)
                    dve.wait_ge(f_t, RING + k + 1)
                    dve.wait_ge(f_mm, k + 1)
                    dve.tensor_copy(xft[:, b, :, :], ps[:, b, :].rearrange("p (c n) -> p c n", c=CHUNKS)).then_inc(f_xt, 1)

            dve.wait_ge(f_end, 1)
            dve.tensor_scalar(xf[0:EXPERTS, 0, 0:FF], ps[0:EXPERTS, 6, 0:FF], es[0:EXPERTS, 5:6], None,
                              ALU.mult).then_inc(g_mean, 1)
            dve.wait_ge(g_trs, 1)
            diag = xf[:, 1, 0:2 * EXPERTS * EXPERTS].rearrange("p (c e f) -> p c e f", c=2, e=EXPERTS)
            ln = Count(dve, v_link, count)
            eq = erow[:, 0:3, :].rearrange("p a n -> p (a n)")[:, 0:EXPERTS * EXPERTS].rearrange("p (e f) -> p e f", e=EXPERTS)
            ln.link(dve.tensor_tensor(eq, pick[:, :].unsqueeze(2).to_broadcast([P, EXPERTS, EXPERTS]),
                                      pick[:, :].unsqueeze(1).to_broadcast([P, EXPERTS, EXPERTS]), ALU.is_equal))
            for c in range(FF // P):
                last = dve.tensor_tensor(diag[:, c, :, :], eq,
                                         hid[:, 0, c * EXPERTS:(c + 1) * EXPERTS].unsqueeze(2).to_broadcast([P, EXPERTS, EXPERTS]),
                                         ALU.mult)
            last.then_inc(g_diag, 1)
            dve.wait_ge(g_y, 1)
            dve.tensor_copy(xf[0:EXPERTS, 2, :], ps[0:EXPERTS, 0, :]).then_inc(g_ys, 1)
            count += ln.n

            def mix(it, n, rows):
                ln = Count(dve, v_link, count + it * UNROLL)
                r = slice(0, rows)

                def weights(b):
                    i = UNROLL * it + b
                    dve.wait_ge(g_rt, reuse(i, 2))
                    ln.link(dve.tensor_scalar(hotk[r, b % 2:b % 2 + 1, :], first[r, ds(i, 1), :], top[r, 0, ds(i, 1)], None, ALU.mult))
                    dve.scalar_tensor_tensor(hotk[r, b % 2:b % 2 + 1, :], second[r, ds(i, 1), :], top[r, 1, ds(i, 1)],
                                             hotk[r, b % 2:b % 2 + 1, :], ALU.mult, ALU.add).then_inc(g_rw, 1)

                def total(b):
                    i = UNROLL * it + b
                    dve.wait_ge(g_o, ready(i))
                    dve.tensor_tensor(agg[r, ds(i, 1), 0:D], agg[r, ds(i, 1), 0:D], ps[r, 3 + b % 2, :].unsqueeze(1),
                                      ALU.add).then_inc(g_x, 1)

                weights(0)
                for b in range(1, n):
                    weights(b)
                    total(b - 1)
                total(n - 1)
                assert ln.n == n

            rounds(dve, mix)


def pickup(dve, iota_row, p, slots, experts):
    return iota_row[:, 1:experts + 1].unsqueeze(1).to_broadcast([p, slots, experts])


def kernel(x, src, dst, L0_gnn_W_self, L0_gnn_b_self, L0_gnn_W_neigh, L0_gnn_gamma, L0_gnn_beta, L0_gnn_alpha,
           L0_ffn_gate_weight, L0_ffn_w1, L0_ffn_w2):
    import numpy as np
    import concourse.bacc as bacc
    from concourse.bass_utils import run_bass_kernel_spmd

    arrays = {
        "x": x, "src": src, "dst": dst,
        "w_self": L0_gnn_W_self, "b_self": np.asarray(L0_gnn_b_self).reshape(1, D), "w_neigh": L0_gnn_W_neigh,
        "gamma": np.asarray(L0_gnn_gamma).reshape(1, D), "beta": np.asarray(L0_gnn_beta).reshape(1, D),
        "alpha": np.asarray(L0_gnn_alpha).reshape(1, 1),
        "gate_t": np.asarray(L0_ffn_gate_weight).T,
        "w1_t": np.asarray(L0_ffn_w1).reshape(EXPERTS * FF, D).T,
        "w2_t": np.asarray(L0_ffn_w2).transpose(0, 2, 1),
    }
    arrays = {f"in_{n}": np.ascontiguousarray(a) for n, a in arrays.items()}
    nc = bacc.Bacc("TRN2", target_bir_lowering=False, num_devices=1)
    args = [nc.dram_tensor(n, a.shape, mybir.dt.from_np(a.dtype), kind="ExternalInput").ap() for n, a in arrays.items()]
    args.append(nc.dram_tensor("out_x", (N, D), mybir.dt.float32, kind="ExternalOutput").ap())
    build(nc, *args)
    r = run_bass_kernel_spmd(nc, [arrays], core_ids=[0])
    return r.results[0]["out_x"]
```

```python
import concourse.bass as bass
from concourse import mybir
from contextlib import ExitStack

P = 128
N, D, EXPERTS, FF = 6250, 512, 16, 256
EDGES = 106250
CHUNKS = D // P
TILES = -(-N // P)
TAIL = N - (TILES - 1) * P
HALF = 4
UNROLL = 2 * HALF
ROUNDS = (TILES - 1) // UNROLL
EDGE_TILES = -(-EDGES // P)
EDGE_CHUNKS = -(-EDGE_TILES // P)
STEPS = EDGE_TILES + TILES
SHALF = 8
BODY = 2 * SHALF
STEP_ROUNDS = STEPS // BODY
SLOTS = -(-2 * N // P) + EXPERTS
RING = 3
CAP = (TILES + 1) * P
DUMMY = EXPERTS * CAP
SCALE = 1024.0
TOP = 2.0 ** 13
EPS = 1e-5
CREDIT = UNROLL
assert STEPS % BODY == 0 and TILES == UNROLL * ROUNDS + 1 and SLOTS % RING == 0


def ready(i):
    return CREDIT + i + 1


def reuse(i, ring):
    return CREDIT - ring + i + 1


def masks(q, n):
    return HALF * q + n


class Count:

    def __init__(self, eng, sem, start):
        self.eng, self.sem, self.start, self.n = eng, sem, start, 0

    def link(self, ins):
        ins.then_inc(self.sem, 1)
        self.n += 1
        self.eng.wait_ge(self.sem, self.start + self.n)


class Part:

    def __init__(self, q, par, n=HALF, rows=P):
        self.q, self.par, self.n, self.rows = q, par, n, rows

    def tile(self, b):
        return HALF * self.q + b


def build(nc, x, src, dst, w_self, b_self, w_neigh, gamma, beta, alpha, gate_t, w1_t, w2_t, out):
    f32, f16, bf16, i32 = mybir.dt.float32, mybir.dt.float16, mybir.dt.bfloat16, mybir.dt.int32
    ALU = mybir.AluOpType
    ACT = mybir.ActivationFunctionType
    X = mybir.AxisListType.X
    ds = bass.ds

    ctx = ExitStack()
    with ctx:
        def sem(name):
            return ctx.enter_context(nc.semaphore(name))

        def sems(name, n):
            return [sem(f"{name}{i}") for i in range(n)]

        def sb(name, shape, dt=f32):
            return ctx.enter_context(nc.sbuf_tensor(name, shape, dt))

        table = nc.dram_tensor("table", [N, 2 * D], f16).ap()
        self_d = nc.dram_tensor("self_d", [TILES * P, D], f32).ap()
        resid_d = nc.dram_tensor("resid_d", [TILES * P, D], f32).ap()
        bucket = nc.dram_tensor("bucket", [DUMMY + P, 2 * D], f16).ap()
        w1_parts = nc.dram_tensor("w1_parts", [EXPERTS * P, CHUNKS * 2 * FF], f16).ap()

        agg = sb("agg", [P, TILES, D + 1])
        wparts = sb("wparts", [P, 2, 2, CHUNKS, D], f16)
        wsp, wnp = wparts[:, 0, :, :, :], wparts[:, 1, :, :, :]
        gwp = sb("gwp", [P, 2, CHUNKS, EXPERTS], f16)
        gammab = sb("gammab", [P, D])
        betab = sb("betab", [P, D])
        alphab = sb("alphab", [P, 1])
        minus_alpha = sb("minus_alpha", [P, 1])
        ident = sb("ident", [P, P])
        identh = sb("identh", [P, P], f16)
        identb = sb("identb", [P, P], bf16)
        ones = sb("ones", [P, P])
        before = sb("before", [P, EXPERTS + 1])
        before16 = sb("before16", [P, P], bf16)
        ones16 = sb("ones16", [P, P], bf16)
        onesh = sb("onesh", [P, 1], f16)
        shift = sb("shift", [EXPERTS, EXPERTS + 1])
        iota_row = sb("iota_row", [P, P])
        iota_p = sb("iota_p", [P, EDGE_CHUNKS])
        pick = sb("pick", [P, EXPERTS])
        ecap = sb("ecap", [P, EXPERTS])
        rstd = sb("rstd", [P, TILES])
        nmr = sb("nmr", [P, TILES])
        inv = sb("inv", [P, TILES])
        first = sb("first", [P, TILES, EXPERTS], bf16)
        second = sb("second", [P, TILES, EXPERTS], bf16)
        top = sb("top", [P, 2, TILES])
        stats = sb("stats", [P, UNROLL, 6])
        mv = sb("mv", [P, 2 * UNROLL, 2])
        var = sb("var", [P, UNROLL])
        guess = sb("guess", [P, UNROLL])
        fix = sb("fix", [P, UNROLL])
        gs = sb("gs", [P, 2, UNROLL])
        gb = sb("gb", [P, 2, UNROLL])
        wmax = sb("wmax", [P, 3 + EXPERTS])
        wpow = sb("wpow", [4, 16])
        wscale = sb("wscale", [P, 8])

        WORK = 18320
        work = sb("work", [P, WORK])
        place = [0]

        def cut(words, start=None):
            if start is not None:
                place[0] = start
            a = place[0]
            place[0] += words
            assert place[0] <= WORK, place[0]
            return work[:, a:a + words]

        xin = cut(UNROLL * D, 0).rearrange("p (b n) -> p b n", b=UNROLL)
        xs = cut(HALF * D).rearrange("p (b n) -> p b n", b=HALF)
        tb = cut(UNROLL * D).bitcast(f16).rearrange("p (b n) -> p b n", b=UNROLL)
        KW = STEPS + BODY
        idx_all = cut(KW, WORK - 3 * KW).bitcast(i32)
        dstrel = cut(KW)
        jrow = cut(KW).bitcast(i32)
        scratch = agg[:, :, :].rearrange("p t n -> p (t n)")
        b_at = [0]

        def cut_b(words):
            b_at[0] += words
            return scratch[:, b_at[0] - words:b_at[0]]

        srci = cut_b(EDGE_CHUNKS * P).bitcast(i32).rearrange("p (c e) -> p c e", c=EDGE_CHUNKS)
        dsti = cut_b(EDGE_CHUNKS * P).bitcast(i32).rearrange("p (c e) -> p c e", c=EDGE_CHUNKS)
        srcf = cut_b(EDGE_CHUNKS * P).rearrange("p (c e) -> p c e", c=EDGE_CHUNKS)
        dstf = cut_b(EDGE_CHUNKS * P).rearrange("p (c e) -> p c e", c=EDGE_CHUNKS)
        most = cut_b(EDGE_CHUNKS)
        bounds = cut_b(TILES - 1)
        passed = cut_b(EDGE_CHUNKS * (TILES - 1)).rearrange("p (c j) -> p c j", c=EDGE_CHUNKS)
        turn = cut_b(1)
        kvals = cut_b(STEPS)
        later = cut_b(STEPS)
        jall = cut_b(STEPS)
        tall = cut_b(STEPS)
        hit = cut_b(2 * STEPS).rearrange("p (a k) -> p a k", a=2)
        DIRTY = -(-b_at[0] // (D + 1))
        gath = cut(SHALF * D, 0).bitcast(f16).rearrange("p (b n) -> p b n", b=SHALF)
        hot = cut(BODY * P // 2).bitcast(f16).rearrange("p (h b n) -> p h b n", h=2, b=SHALF)
        idxb = cut(BODY).bitcast(i32)
        cx = cut(D)
        cxp = cut(D).bitcast(f16)
        cxn = cut(D)
        cxt = cut(D).bitcast(f16).rearrange("p (a c n) -> p a c n", a=2, c=CHUNKS)
        cs = cut(D)
        cr = cut(D)
        stage = cut(CHUNKS * FF).rearrange("p (c n) -> p c n", c=CHUNKS)
        staged = cut(CHUNKS * FF).bitcast(f16).rearrange("p (c a n) -> p c a n", c=CHUNKS, a=2)
        wst = cut((2 * D + EXPERTS) * CHUNKS)
        ws, wn, gw = (wst[:, a * CHUNKS:b * CHUNKS].rearrange("p (c n) -> p c n", c=CHUNKS)
                      for a, b in ((0, D), (D, 2 * D), (2 * D, 2 * D + EXPERTS)))
        bself = cut(D)
        assert place[0] <= WORK - 3 * KW
        D_AT = WORK - 11130
        scaled = cut(2 * D, D_AT).rearrange("p (b n) -> p b n", b=2)
        aggt = cut(2 * D).bitcast(f16).rearrange("p (b a c n) -> p b a c n", b=2, a=2, c=CHUNKS)
        sbuf = cut(2 * D).rearrange("p (b n) -> p b n", b=2)
        rbuf = cut(2 * D).rearrange("p (b n) -> p b n", b=2)
        below = cut(2 * D).rearrange("p (b n) -> p b n", b=2)
        x2f = cut(2 * D).rearrange("p (b n) -> p b n", b=2)
        x2 = cut(HALF * D).bitcast(f16).rearrange("p (b n) -> p b n", b=HALF)
        x2t = cut(2 * D).bitcast(f16).rearrange("p (b a c n) -> p b a c n", b=2, a=2, c=CHUNKS)
        GE = HALF * EXPERTS

        def small():
            return cut(GE).rearrange("p (b e) -> p b e", b=HALF)

        logit, cand, logit2, spot, prod, pickf = small(), small(), small(), small(), small(), small()
        lead = cut(HALF)
        row = cut(4 * HALF).bitcast(i32).rearrange("p (h k b) -> p h k b", h=2, k=2)
        rowf = cut(2 * HALF).rearrange("p (k b) -> p k b", k=2)
        mask = cut(GE // 2).bitcast(bf16).rearrange("p (b e) -> p b e", b=HALF)
        run = cut((HALF + 1) * EXPERTS // 2).bitcast(bf16).rearrange("p (b e) -> p b e", b=HALF + 1)
        w1 = cut(CHUNKS * EXPERTS * FF, 0).bitcast(f16).rearrange("p (e c a n) -> p e c a n", e=EXPERTS, c=CHUNKS, a=2)
        W1E = CHUNKS * FF
        EARLY = D_AT // W1E
        hid = cut(RING * FF).rearrange("p (b n) -> p b n", b=RING)
        hotk = cut(RING * EXPERTS).rearrange("p (b n) -> p b n", b=RING)
        hote = cut(SLOTS * EXPERTS // 2).bitcast(f16).rearrange("p (k e) -> p k e", k=SLOTS)
        old = wparts[:, :, :, :, :].rearrange("p w a c n -> p (w a c n)")
        xf = old[:, 0:RING * 2 * D].rearrange("p (b n) -> p b n", b=RING)
        xft = old[:, RING * 2 * D:2 * RING * 2 * D].rearrange("p (b a c n) -> p b a c n", b=RING, a=2, c=CHUNKS)
        rowk = sb("rowk", [1, SLOTS], i32)
        expk = sb("expk", [1, SLOTS], i32)
        fillrow = sb("fillrow", [1, EXPERTS], i32)
        es = sb("es", [P, 8])
        steps49 = sb("steps49", [EXPERTS, TILES])
        reach = sb("reach", [EXPERTS + 1, SLOTS])
        erow = gammab[:, 0:4 * SLOTS].rearrange("p (a k) -> p a k", a=4)
        mixw = sb("mixw", [P, 2, TILES, EXPERTS])
        w2 = cut(EXPERTS * 2 * D, 0).rearrange("p (e c n) -> p e c n", e=EXPERTS, c=2)
        es2, mixt = cut(2 * EXPERTS), cut(P).bitcast(bf16).rearrange("p (b n) -> p b n", b=2)
        yp = cut(D).bitcast(bf16).rearrange("p (a n) -> p a n", a=2)
        ystack, ylow = cut(D // 2).bitcast(bf16), cut(D)
        STACKED = TILES * 8 * EXPERTS
        stack = old[:, 0:STACKED].bitcast(bf16).rearrange("p (t n) -> p t n", t=TILES)
        after = old[:, STACKED:STACKED + 4 * 448].bitcast(f32)
        diag = after[:, 0:512].rearrange("p (c e f) -> p c e f", c=2, e=EXPERTS)
        same = after[:, 512:768].rearrange("p (e f) -> p e f", e=EXPERTS)
        rep = after[0:EXPERTS, 768:896]
        zero = sb("zero", [P, D])
        spare = mixw[0:EXPERTS, 1, :, :].rearrange("p t e -> p (t e)")
        mean, y16 = spare[:, 0:FF], spare[:, FF:FF + D]

        ps = ctx.enter_context(nc.psum_tensor("ps", [P, 8, 512], f32))

        def bank16(b, dt=f16):
            return ps[:, b, :].bitcast(dt)

        s_const, s_zero, s_edge, s_pad = sem("s_const"), sem("s_zero"), sem("s_edge"), sem("s_pad")
        a_x, a_st = sems("a_x", UNROLL), sems("a_st", UNROLL)
        a_stat, a_norm, a_lo = sem("a_stat"), sem("a_norm"), sem("a_lo")
        b_cmp, b_cnt, b_later, b_jb, b_hit, b_acc, b_done = [sem(f"b_{n}") for n in
                                                             ("cmp", "cnt", "later", "jb", "hit", "acc", "done")]
        w_max, w_tr, w_diag, w_bc, w_scale, w_hi, w_lo = [sem(f"w_{n}") for n in
                                                          ("max", "tr", "diag", "bc", "scale", "hi", "lo")]
        v_ld, v_max, v_hi, v_lo, v_st = [sem(f"v_{n}") for n in ("ld", "max", "hi", "lo", "st")]
        c_g = sems("c_g", SHALF)
        c_step, c_sum, c_hot, c_idx = sem("c_step"), sem("c_sum"), sem("c_hot"), sem("c_idx")
        c_x, c_xp, c_xn, c_r, c_t, c_xt, c_mm, c_s, c_rs, c_ss = [sem(f"c_{n}") for n in
                                                                  ("x", "xp", "xn", "r", "t", "xt", "mm", "s", "rs", "ss")]
        d_s, d_r = sems("d_s", 2), sems("d_r", 2)
        d_inv, d_sc, d_t, d_hi, d_lo, d_mm, d_h = [sem(f"d_{n}") for n in ("inv", "sc", "t", "hi", "lo", "mm", "h")]
        d_stat, d_hn, d_gm, d_bt, d_pr, d_lk, d_x1 = [sem(f"d_{n}") for n in ("stat", "hn", "gm", "bt", "pr", "lk", "x1")]
        d_x2, d_x2l, d_t2, d_xt = [sem(f"d_{n}") for n in ("x2", "x2l", "t2", "xt")]
        d_lg, d_mask, d_pos, d_row = [sem(f"d_{n}") for n in ("lg", "mask", "pos", "row")]
        d_sc1, d_sc2 = sems("d_sc1", HALF), sems("d_sc2", HALF)
        e_w1 = sem("e_w1")
        e_cnt, e_n, e_base, e_reach, e_list, e_done, e_fill = [sem(f"e_{n}") for n in
                                                               ("cnt", "n", "base", "reach", "list", "done", "fill")]
        f_x = sems("f_x", RING)
        f_t, f_xt, f_mm, f_hid, f_hot, f_acc, f_end = [sem(f"f_{n}") for n in
                                                      ("t", "xt", "mm", "hid", "hot", "acc", "end")]
        g_w2 = sems("g_w2", 4)
        g_mean, g_tr, g_trs, g_diag, g_y, g_ys, g_rep, g_yst = [sem(f"g_{n}") for n in
                                                               ("mean", "tr", "trs", "diag", "y", "ys", "rep", "yst")]
        g_ex, g_exd, g_soft, g_mixw, g_rt, g_rts, g_o, g_x, g_out = [sem(f"g_{n}") for n in
                                                                     ("ex", "exd", "soft", "mixw", "rt", "rts", "o", "x", "out")]
        v_link, r_link, k_link, p_link, q_link = sem("v_link"), sem("r_link"), sem("k_link"), sem("p_link"), sem("q_link")

        def rounds(eng, body):
            with eng.Fori(0, ROUNDS) as it:
                body(it, UNROLL, P)
            body(ROUNDS, 1, TAIL)

        def halves(it, n, rows):
            return [Part(2 * it + h, h, min(HALF, n - h * HALF), rows) for h in range(-(-n // HALF))]

        LAST = 2 * ROUNDS

        def pipeline(eng, step):
            tail = Part(LAST, 0, 1, TAIL)
            step(Part(0, 0), None, None)
            step(Part(1, 1), Part(0, 0), None)
            with eng.Fori(0, ROUNDS - 1) as it:
                step(Part(2 * it + 2, 0), Part(2 * it + 1, 1), Part(2 * it, 0))
                step(Part(2 * it + 3, 1), Part(2 * it + 2, 0), Part(2 * it + 1, 1))
            step(tail, Part(LAST - 1, 1), Part(LAST - 2, 0))
            step(None, tail, Part(LAST - 1, 1))
            step(None, None, tail)

        def beside(eng, body):
            with eng.Fori(0, EXPERTS) as it:
                body(it, P, "max")
            with eng.Fori(EXPERTS, 2 * EXPERTS) as it:
                body(it, P, "split")
            with eng.Fori(2 * EXPERTS, TILES - 1) as it:
                body(it, P, None)
            body(TILES - 1, TAIL, None)
            with eng.Fori(TILES, STEP_ROUNDS) as it:
                body(it, 0, None)

        def chunks16(a, rows):
            return a.rearrange("p (a c n) -> p a c n", a=2, c=CHUNKS)[:, :, :, 0:rows]

        block = ctx.enter_context(nc.Block())

        @block.sync
        def _(sp):
            full = (EDGE_CHUNKS - 1) * P * P
            rows_left = (EDGES - full) // P
            rest = EDGES - full - rows_left * P
            for a, t in ((src, srci), (dst, dsti)):
                sp.dma_start(t[:, 0:EDGE_CHUNKS - 1, :],
                             a[0:full].rearrange("(c p e) -> p c e", p=P, e=P)).then_inc(s_edge, 16)
            sp.wait_ge(s_pad, 2)
            for a, t in ((src, srci), (dst, dsti)):
                sp.dma_start(t[0:rows_left, EDGE_CHUNKS - 1, :],
                             a[full:full + rows_left * P].rearrange("(p e) -> p e", e=P)).then_inc(s_edge, 16)
                sp.dma_start(t[rows_left:rows_left + 1, EDGE_CHUNKS - 1, 0:rest],
                             a[full + rows_left * P:EDGES].rearrange("(p e) -> p e", p=1)).then_inc(s_edge, 16)

            def load_x(it, b, rows):
                i = UNROLL * it + b
                sp.wait_ge(a_norm, reuse(i, UNROLL))
                sp.dma_start(xin[0:rows, b, :], x[ds(i * P, rows), :]).then_inc(a_x[b], 16)

            def store_table(it, b, rows):
                i = UNROLL * it + b
                sp.wait_ge(a_lo, ready(i))
                sp.dma_start(table[ds(i * P, rows), :], tb[0:rows, b, :]).then_inc(a_st[b], 16)

            for b in range(UNROLL):
                load_x(0, b, P)
            first_use = ((gammab[:, :], gamma.to_broadcast([P, D])), (betab[:, :], beta.to_broadcast([P, D])),
                         (alphab[:, :], alpha.to_broadcast([P, 1])), (bself[:, :], b_self.to_broadcast([P, D])),
                         (gw[:, 0:1, :], gate_t[0:P, :].unsqueeze(1)), (gw[:, 1:2, :], gate_t[P:2 * P, :].unsqueeze(1)),
                         (gw[:, 2:3, :], gate_t[2 * P:3 * P, :].unsqueeze(1)), (gw[:, 3:4, :], gate_t[3 * P:4 * P, :].unsqueeze(1)))
            for b, (to, what) in enumerate(first_use):
                sp.dma_start(to, what).then_inc(a_st[b], 16)
            with sp.Fori(0, ROUNDS - 1) as it:
                for b in range(UNROLL):
                    load_x(it + 1, b, P)
                    store_table(it, b, P)
            load_x(ROUNDS, 0, TAIL)
            for b in range(UNROLL):
                store_table(ROUNDS - 1, b, P)
            store_table(ROUNDS, 0, TAIL)
            sp.dma_start(wn[:, :, :], w_neigh.rearrange("(c p) n -> p c n", p=P)).then_inc(v_st, 16)
            sp.dma_start(ws[:, 0:2, :], w_self[0:2 * P, :].rearrange("(c p) n -> p c n", p=P)).then_inc(c_ss, 16)
            sp.dma_start(ws[:, 2:4, :], w_self[2 * P:, :].rearrange("(c p) n -> p c n", p=P)).then_inc(c_rs, 16)
            for b in range(UNROLL):
                sp.wait_ge(a_st[b], 16 * (1 + ROUNDS + (b == 0)))

            def side(it, rows, w1_turn):
                if w1_turn == "max":
                    sp.wait_ge(v_max, it + 1)
                    sp.dma_start(stage[:, :, :], w1_t[:, ds(it * FF, FF)].rearrange("(c p) n -> p c n", p=P)).then_inc(v_ld, 16)
                elif w1_turn == "split":
                    sp.wait_ge(v_max, EXPERTS + 1)
                    sp.wait_ge(v_lo, it - EXPERTS + 1)
                    sp.dma_start(stage[:, :, :], w1_t[:, ds((it - EXPERTS) * FF, FF)].rearrange("(c p) n -> p c n", p=P)
                                 ).then_inc(v_ld, 16)
                if not rows:
                    return
                i = it
                sp.wait_ge(c_r, i + 1)
                sp.dma_start(cx[0:rows, :], x[ds(i * P, rows), :]).then_inc(c_x, 16)
                sp.wait_ge(c_t, i + 1)
                sp.dma_start(cxp[0:rows, :], table[ds(i * P, rows), :]).then_inc(c_xp, 16)
                sp.wait_ge(c_r, i + 2)
                sp.dma_start(resid_d[ds(i * P, rows), :], cr[0:rows, :]).then_inc(c_rs, 16)
                if w1_turn == "split":
                    sp.wait_ge(v_lo, it - EXPERTS + 2)
                    sp.dma_start(w1_parts[ds((it - EXPERTS) * P, P), :], staged[:, :, :, :].rearrange("p c a n -> p (c a n)")
                                 ).then_inc(v_st, 16)
                sp.wait_ge(c_s, i + 2)
                sp.dma_start(self_d[ds(i * P, rows), :], cs[0:rows, :]).then_inc(c_ss, 16)

            beside(sp, side)

            sp.wait_ge(c_ss, 16 * (TILES + 1))
            sp.wait_ge(c_rs, 16 * (TILES + 1))
            sp.wait_ge(v_st, 16 * (EXPERTS + 1))
            sp.wait_ge(d_inv, 1)

            def load_w1(lo, hi):
                for e in range(lo, hi):
                    sp.dma_start(w1[:, e, :, :, :].rearrange("p c a n -> p (c a n)"), w1_parts[e * P:(e + 1) * P, :]).then_inc(e_w1, 16)

            def load_d(nxt, cur, prev):
                if nxt:
                    for b in range(nxt.n):
                        i = nxt.tile(b)
                        sp.wait_ge(d_h, reuse(i, 2))
                        sp.dma_start(sbuf[0:nxt.rows, b % 2, :], self_d[ds(i * P, nxt.rows), :]).then_inc(d_s[b % 2], 16)
                        if cur and b < cur.n:
                            load_r(cur, b)
                    if cur is None and prev is None:
                        load_w1(0, EARLY)
                elif cur:
                    load_r(cur, 0)

            def load_r(part, b):
                i = part.tile(b)
                sp.wait_ge(d_x1, reuse(i, 2))
                sp.dma_start(rbuf[0:part.rows, b % 2, :], resid_d[ds(i * P, part.rows), :]).then_inc(d_r[b % 2], 16)

            def load_step(nxt, cur, prev):
                load_d(nxt, cur, prev)
                if nxt and cur:
                    for b in range(nxt.n, cur.n):
                        load_r(cur, b)

            pipeline(sp, load_step)

            sp.wait_ge(e_cnt, 1)
            for b in range(HALF):
                sp.wait_ge(d_sc1[b], 16 * (1 + LAST + (b == 0)))
                sp.wait_ge(d_sc2[b], 16 * (1 + LAST + (b == 0)))
            load_w1(EARLY, EXPERTS)
            sp.wait_ge(e_n, 1)
            zeros = zero[:, :].bitcast(f16)
            for e in range(EXPERTS):
                at = sp.value_load(fillrow[0:1, e:e + 1], min_val=e * CAP, max_val=e * CAP + N)
                sp.dma_start(bucket[ds(at, P), :], zeros).then_inc(e_fill, 16)
            sp.wait_ge(e_fill, 16 * EXPERTS)
            sp.wait_ge(e_done, 1)

            with sp.Fori(0, SLOTS // RING) as it:
                for b in range(RING):
                    k = RING * it + b
                    at = sp.value_load(rowk[0:1, ds(k, 1)], min_val=0, max_val=DUMMY)
                    sp.wait_ge(f_t, k + 1)
                    sp.dma_start(xf[:, b, :], bucket[ds(at, P), :]).then_inc(f_x[b], 16)

            sp.wait_ge(f_mm, SLOTS + RING)
            for e in range(EXPERTS):
                sp.dma_start(w2[:, e, :, :], w2_t[e, :, :].rearrange("(c p) n -> p c n", p=P)).then_inc(g_w2[e // 4], 16)

            def store_out(it, n, rows):
                for b in range(n):
                    i = UNROLL * it + b
                    sp.wait_ge(g_x, ready(i))
                    sp.dma_start(out[ds(i * P, rows), :], agg[0:rows, ds(i, 1), 0:D]).then_inc(g_out, 16)

            rounds(sp, store_out)
            sp.wait_ge(g_out, 16 * TILES)

        @block.gpsimd
        def _(pool):
            ln = Count(pool, p_link, 0)
            loose = dict(allow_small_or_imprecise_dtypes=True)
            pool.memset(srci[:, EDGE_CHUNKS - 1, :], 0).then_inc(s_pad, 1)
            pool.memset(dsti[:, EDGE_CHUNKS - 1, :], -1).then_inc(s_pad, 1)
            pool.memset(ones[:, :], 1.0)
            ln.link(pool.memset(ones16[:, :], 1.0))
            pool.iota(iota_row[:, :], pattern=[[1, P]], base=0, channel_multiplier=0, **loose)
            pool.iota(iota_p[:, :], pattern=[[P, EDGE_CHUNKS]], base=0, channel_multiplier=1, **loose)
            pool.iota(bounds[:, :], pattern=[[P, TILES - 1]], base=P, channel_multiplier=0, **loose)
            pool.iota(kvals[:, :], pattern=[[1, STEPS]], base=0, channel_multiplier=0, **loose).then_inc(s_const, 1)
            pool.memset(onesh[:, :], 1.0)
            pool.memset(top[:, :, :], 0.0)
            pool.memset(first[:, :, :], 0.0)
            pool.memset(second[:, :, :], 0.0)
            pool.memset(mv[:, :, :], 1.0)
            pool.iota(pick[:, :], pattern=[[-1, EXPERTS]], base=EXPERTS, channel_multiplier=0, **loose)
            pool.iota(ecap[:, :], pattern=[[CAP, EXPERTS]], base=0, channel_multiplier=0, **loose)
            pool.iota(steps49[:, :], pattern=[[P, TILES]], base=0, channel_multiplier=0, **loose)
            ln.link(pool.affine_select(out=ident[:, :], in_=ones[:, :], compare_op=ALU.is_equal, fill=0.0, base=0,
                                       pattern=[[-1, P]], channel_multiplier=1))
            pool.tensor_copy(identh[:, :], ident[:, :])
            pool.tensor_copy(identb[:, :], ident[:, :])
            pool.affine_select(out=before[:, :], in_=ones[:, 0:EXPERTS + 1], compare_op=ALU.is_gt, fill=0.0, base=0,
                               pattern=[[1, EXPERTS + 1]], channel_multiplier=-1)
            pool.affine_select(out=before16[:, :], in_=ones16[:, :], compare_op=ALU.is_gt, fill=0.0, base=0,
                               pattern=[[1, P]], channel_multiplier=-1)
            pool.affine_select(out=shift[:, :], in_=ones[0:EXPERTS, 0:EXPERTS + 1], compare_op=ALU.is_equal, fill=0.0,
                               base=-1, pattern=[[1, EXPERTS + 1]], channel_multiplier=-1).then_inc(s_const, 1)
            pool.memset(zero[:, :], 0.0)
            pool.memset(agg[:, DIRTY:TILES, :], 0.0).then_inc(s_zero, 1)
            for s in (a_lo, d_gm, d_bt, d_x2l):
                pool.sem_inc(s, CREDIT)

            def low(it, n, rows):
                for b in range(n):
                    i = UNROLL * it + b
                    pool.wait_ge(a_norm, ready(i))
                    pool.tensor_tensor(tb[0:rows, b, D:2 * D], xs[0:rows, b % HALF, :], tb[0:rows, b, 0:D],
                                       ALU.subtract).then_inc(a_lo, 1)

            rounds(pool, low)

            for b in range(UNROLL):
                pool.wait_ge(a_st[b], 16 * (1 + ROUNDS + (b == 0)))

            def gathers(it, rows, w1_turn):
                for s in range(BODY):
                    if s % SHALF == 0:
                        pool.wait_ge(c_idx, 2 * it + s // SHALF + 1)
                    pool.wait_ge(c_step, BODY * it + s + 1 + SHALF)
                    pool.nop(nofuse=True)
                    pool.indirect_dma_start(
                        out=gath[:, s % SHALF, :], out_offset=None, in_=table[:, :],
                        in_offset=bass.IndirectOffsetOnAxis(ap=idxb[:, s:s + 1], axis=0)).then_inc(c_g[s % SHALF], 16)

            with pool.Fori(0, STEP_ROUNDS) as it:
                gathers(it, 0, None)

            share = P // (2 * HALF)
            for n, done in enumerate(d_sc1 + d_sc2):
                pool.dma_start(bucket[DUMMY + n * share:DUMMY + (n + 1) * share, :],
                               zero[n * share:(n + 1) * share, :].bitcast(f16)).then_inc(done, 16)

            def route(nxt, cur, prev):
                if nxt:
                    r = slice(0, nxt.rows)
                    for b in range(nxt.n):
                        i = nxt.tile(b)
                        slot = agg[r, ds(i, 1), 0:D]
                        pool.wait_ge(d_hn, ready(i))
                        pool.nop(nofuse=True)
                        pool.tensor_tensor(slot, slot, gammab[r, :].unsqueeze(1), ALU.mult).then_inc(d_gm, 1)
                    for b in range(nxt.n):
                        i = nxt.tile(b)
                        slot = agg[r, ds(i, 1), 0:D]
                        pool.wait_ge(d_gm, ready(i))
                        pool.nop(nofuse=True)
                        pool.tensor_tensor(slot, slot, betab[r, :].unsqueeze(1), ALU.add).then_inc(d_bt, 1)
                if prev:
                    pool.wait_ge(d_row, prev.q + 1)
                    pool.nop(nofuse=True)
                    for b in range(prev.n):
                        for k, done in ((0, d_sc1), (1, d_sc2)):
                            pool.indirect_dma_start(
                                out=bucket[:, :], in_=x2[0:prev.rows, b, :], in_offset=None,
                                out_offset=bass.IndirectOffsetOnAxis(ap=row[0:prev.rows, prev.par, k, b:b + 1], axis=0),
                            ).then_inc(done[b], 16)
                if cur:
                    for b in range(cur.n):
                        i = cur.tile(b)
                        pool.wait_ge(d_x2, ready(i))
                        pool.tensor_tensor(x2[0:cur.rows, b, D:2 * D], x2f[0:cur.rows, b % 2, :],
                                           x2[0:cur.rows, b, 0:D], ALU.subtract).then_inc(d_x2l, 1)

            pipeline(pool, route)

            pool.wait_ge(g_soft, 1)
            wide = lambda k: top[:, k, :].unsqueeze(2).to_broadcast([P, TILES, EXPERTS])
            for k, pickd in enumerate((first, second)):
                last = pool.tensor_tensor(mixw[:, k, :, :], pickd[:, :, :], wide(k), ALU.mult)
            lq = Count(pool, q_link, 0)
            lq.link(last)
            pool.tensor_tensor(mixw[:, 0, :, :], mixw[:, 0, :, :], mixw[:, 1, :, :], ALU.add).then_inc(g_mixw, 1)

        @block.scalar
        def _(act):
            for s in (a_norm, d_sc, d_hi, d_hn, d_pr, d_x2, d_xt, g_rts):
                act.sem_inc(s, CREDIT)
            act.sem_inc(c_xt, 1)
            act.sem_inc(f_hid, RING)

            def norm(it, n, rows):
                for part in halves(it, n, rows):
                    act.wait_ge(a_stat, part.q + 1)
                    for m in range(part.n):
                        b = part.par * HALF + m
                        i = part.tile(m)
                        act.wait_ge(a_x[b], 16 * (it + 1))
                        act.wait_ge(a_lo, reuse(i, HALF))
                        act.activation(xs[0:rows, m, :], xin[0:rows, b, :], ACT.Identity,
                                       bias=gb[0:rows, 0, b:b + 1], scale=gs[0:rows, 0, b:b + 1])
                        act.wait_ge(a_st[b], 16 * (it + 1))
                        act.activation(tb[0:rows, b, 0:D], xin[0:rows, b, :], ACT.Identity,
                                       bias=gb[0:rows, 0, b:b + 1], scale=gs[0:rows, 0, b:b + 1]).then_inc(a_norm, 1)

            rounds(act, norm)

            act.wait_ge(b_done, 1)

            def index_copy(it, h):
                q = 2 * it + h
                act.wait_ge(c_step, SHALF * q + SHALF)
                act.nop(nofuse=True)
                act.copy(idxb[:, h * SHALF:(h + 1) * SHALF], idx_all[:, ds(SHALF * q, SHALF)]).then_inc(c_idx, 1)

            def side(it, rows, w1_turn):
                index_copy(it, 0)
                index_copy(it, 1)
                if w1_turn == "split":
                    act.wait_ge(w_scale, 2)
                    act.wait_ge(v_ld, 16 * (it + 1))
                    act.wait_ge(v_st, 16 * (it - EXPERTS + 1))
                    act.activation(staged[:, :, 0, :], stage[:, :, :], ACT.Copy, scale=wscale[:, 3:4]).then_inc(v_hi, 1)
                if not rows:
                    return
                i = it
                act.wait_ge(c_x, 16 * (i + 1))
                act.wait_ge(c_r, i + 1)
                act.nop(nofuse=True)
                act.activation(cxn[0:rows, :], cx[0:rows, :], ACT.Identity, bias=nmr[0:rows, ds(i, 1)],
                               scale=rstd[0:rows, ds(i, 1)]).then_inc(c_xn, 1)
                act.wait_ge(c_t, i + 2)
                act.wait_ge(c_mm, i + 1)
                act.copy(cxt[:, :, :, 0:rows], chunks16(bank16(4), rows)).then_inc(c_xt, 1)

            act.wait_ge(w_scale, 1)
            act.activation(wsp[:, 0, :, :], ws[:, :, :], ACT.Copy, scale=wscale[:, 0:1])
            act.activation(wnp[:, 0, :, :], wn[:, :, :], ACT.Copy, scale=wscale[:, 1:2])
            act.activation(gwp[:, 0, :, :], gw[:, :, :], ACT.Copy, scale=wscale[:, 2:3]).then_inc(w_hi, 1)
            beside(act, side)

            act.wait_ge(d_inv, 1)

            def dense(nxt, cur, prev):
                def scale(b):
                    i, r = nxt.tile(b), slice(0, nxt.rows)
                    act.wait_ge(d_t, reuse(i, 2))
                    act.nop(nofuse=True)
                    act.activation(scaled[r, b % 2, :].unsqueeze(1), agg[r, ds(i, 1), 0:D], ACT.Copy,
                                   scale=inv[r, ds(i, 1)]).then_inc(d_sc, 1)

                def high(b):
                    i = nxt.tile(b)
                    act.wait_ge(d_t, ready(i))
                    act.wait_ge(d_mm, reuse(i, 2))
                    act.copy(aggt[:, b % 2, 0, :, 0:nxt.rows],
                             ps[:, b % 2, :].rearrange("p (c n) -> p c n", c=CHUNKS)[:, :, 0:nxt.rows]).then_inc(d_hi, 1)

                def leaky(b):
                    i, r = cur.tile(b), slice(0, cur.rows)
                    slot = agg[r, ds(i, 1), 0:D]
                    act.wait_ge(d_bt, ready(i))
                    act.wait_ge(d_x1, reuse(i, 2))
                    act.nop(nofuse=True)
                    act.activation(below[r, b % 2, :].unsqueeze(1), slot, ACT.Relu, scale=-1.0).then_inc(d_pr, 1)

                if nxt:
                    scale(0)
                    for b in range(nxt.n):
                        if b + 1 < nxt.n:
                            scale(b + 1)
                        high(b)
                        if cur and b < cur.n:
                            leaky(b)
                if cur:
                    for b in range(nxt.n if nxt else 0, cur.n):
                        leaky(b)
                if nxt:
                    act.wait_ge(d_stat, nxt.q + 1)
                    act.nop(nofuse=True)
                    for b in range(nxt.n):
                        i, r, c = nxt.tile(b), slice(0, nxt.rows), b
                        slot = agg[r, ds(i, 1), 0:D]
                        act.activation(slot, slot, ACT.Identity, bias=gb[r, nxt.par, c:c + 1],
                                       scale=gs[r, nxt.par, c:c + 1]).then_inc(d_hn, 1)
                if cur:
                    if not nxt:
                        act.wait_ge(d_stat, cur.q + 2)
                        act.nop(nofuse=True)
                    r = slice(0, cur.rows)

                    def norm2(b):
                        i, c = cur.tile(b), HALF + b
                        act.wait_ge(d_x2l, reuse(i, 2))
                        act.wait_ge(d_sc1[b], 16 * (cur.q + 1))
                        act.wait_ge(d_sc2[b], 16 * (cur.q + 1))
                        act.nop(nofuse=True)
                        slot = agg[r, ds(i, 1), 0:D]
                        act.activation(x2f[r, b % 2, :].unsqueeze(1), slot, ACT.Identity,
                                       bias=gb[r, 1 - cur.par, c:c + 1], scale=gs[r, 1 - cur.par, c:c + 1])
                        act.activation(x2[r, b, 0:D].unsqueeze(1), slot, ACT.Identity,
                                       bias=gb[r, 1 - cur.par, c:c + 1], scale=gs[r, 1 - cur.par, c:c + 1]).then_inc(d_x2, 1)

                    def move_x2(b):
                        i = cur.tile(b)
                        act.wait_ge(d_t2, ready(i))
                        act.wait_ge(d_lg, reuse(i, 2))
                        act.copy(x2t[:, b % 2, :, :, 0:cur.rows], chunks16(bank16(4 + b % 2), cur.rows)).then_inc(d_xt, 1)

                    for b in range(cur.n):
                        norm2(b)
                        if b > 1:
                            move_x2(b - 2)
                    for b in range(max(cur.n - 2, 0), cur.n):
                        move_x2(b)

            pipeline(act, dense)

            act.wait_ge(g_ex, 1)
            act.activation(top[:, 1, :], top[:, 1, :], ACT.Exp, scale=wscale[:, 6:7]).then_inc(g_exd, 1)

            with act.Fori(0, SLOTS // RING) as it:
                for b in range(RING):
                    k = RING * it + b
                    act.wait_ge(f_mm, RING + k + 1)
                    act.wait_ge(f_acc, k + 1)
                    act.activation(hid[:, b, :], ps[:, 3 + b, 0:FF], ACT.Silu, scale=wscale[:, 7:8]).then_inc(f_hid, 1)

            act.wait_ge(g_tr, 1)
            act.copy(es2[:, 0:2 * EXPERTS], ps[:, 7, 0:2 * EXPERTS]).then_inc(g_trs, 1)

            def mix(it, n, rows):
                for b in range(n):
                    i = UNROLL * it + b
                    act.wait_ge(g_rt, ready(i))
                    act.wait_ge(g_o, reuse(i, 2))
                    act.copy(mixt[:, b % 2, 0:rows], ps[:, 1 + b % 2, 0:rows]).then_inc(g_rts, 1)

            rounds(act, mix)

        @block.tensor
        def _(pe):
            for s in (d_t, d_mm, d_t2, d_lg, g_rt, g_o):
                pe.sem_inc(s, CREDIT)
            pe.sem_inc(c_step, BODY)
            pe.sem_inc(c_t, 1)
            pe.sem_inc(c_mm, 1)
            pe.sem_inc(f_mm, RING)
            pe.sem_inc(f_t, RING)
            pe.sem_inc(f_acc, RING)

            NJ = TILES - 1
            pe.wait_ge(s_const, 2)
            pe.wait_ge(b_cmp, 1)
            for c in range(EDGE_CHUNKS):
                last = pe.matmul(ps[0:NJ, 6, 0:1], passed[:, c, :], ones[:, 0:1], start=c == 0,
                                 stop=c == EDGE_CHUNKS - 1)
            last.then_inc(b_cnt, 1)
            pe.wait_ge(b_later, 1)
            H = STEPS // 2
            for h in range(2):
                last = pe.matmul(ps[:, h, 0:H], ones[0:NJ, :], later[0:NJ, h * H:(h + 1) * H], start=True, stop=True)
            last.then_inc(b_jb, 1)
            for c in range(EDGE_CHUNKS):
                pe.wait_ge(b_hit, c + 1)
                for t, bank in ((srcf, 2), (dstf, 4)):
                    for h in range(2):
                        last = pe.matmul(ps[:, bank + h, 0:H], t[:, c, :], hit[:, c % 2, h * H:(h + 1) * H],
                                         start=c == 0, stop=c == EDGE_CHUNKS - 1)
                last.then_inc(b_acc, 1)

            def powers(n, cols, turns):
                pe.wait_ge(w_max, turns)
                pe.transpose(ps[0:n, 6, 0:P], cols, ident[:, :]).then_inc(w_tr, 1)
                pe.wait_ge(w_diag, turns)
                pe.matmul(ps[:, 6, 256:256 + 2 * n], ones[0:n, :], wpow[0:n, 4:4 + 2 * n], start=True, stop=True).then_inc(w_bc, 1)

            powers(3, wmax[:, 0:3], 1)

            pe.wait_ge(b_done, 1)

            def split_mm(to, left, right, n):
                last = None
                for c in range(n):
                    for a, w in ((0, 0), (0, 1), (1, 0)):
                        last = pe.matmul(to, left(a, c), right(w, c), start=c == 0 and a == 0 and w == 0,
                                         stop=c == n - 1 and a == 1)
                return last

            def step(it, s):
                k = BODY * it + s
                b, h = s % SHALF, s // SHALF
                r = 2 * (s % 2)
                if b == 0:
                    pe.wait_ge(c_hot, 2 * it + h + 1)
                pe.wait_ge(c_g[b], 16 * (2 * it + h + 1))
                pe.wait_ge(c_sum, k + 1)
                oh = hot[:, h, b, :]
                pe.matmul(ps[:, r, :], oh, gath[:, b, 0:D], start=True, stop=False)
                pe.matmul(ps[:, r, :], oh, gath[:, b, D:2 * D], start=False, stop=True)
                pe.matmul(ps[:, r + 1, 0:1], oh, onesh[:, :], start=True, stop=True).then_inc(c_step, 1)

            def side_turn(i, rows):
                pe.wait_ge(c_xp, 16 * (i + 1))
                pe.wait_ge(c_xt, i + 1)
                for k in range(2 * CHUNKS):
                    last = pe.transpose(bank16(4)[:, k * P:k * P + rows], cxp[0:rows, k * P:(k + 1) * P], identh[0:rows, 0:rows])
                last.then_inc(c_t, 1)

            def side_project(i, rows):
                pe.wait_ge(c_xt, i + 2)
                pe.wait_ge(c_s, i + 1)
                split_mm(ps[0:rows, 5, :], lambda a, c: cxt[:, a, c, 0:rows], lambda w, c: wsp[:, w, c, :],
                         CHUNKS).then_inc(c_mm, 1)

            def body(it, rows, w1_turn):
                for s in range(BODY):
                    step(it, s)
                    if rows and s == 5:
                        side_turn(it, rows)
                    if rows and s == 10:
                        side_project(it, rows)

            pe.wait_ge(w_lo, 1)
            with pe.Fori(0, EXPERTS) as it:
                body(it, P, "max")
            powers(1, wmax[:, 2:3], 2)
            with pe.Fori(EXPERTS, TILES - 1) as it:
                body(it, P, None)
            body(TILES - 1, TAIL, None)
            with pe.Fori(TILES, STEP_ROUNDS) as it:
                body(it, 0, None)

            pe.wait_ge(d_inv, 1)

            def dense(nxt, cur, prev):
                def turn_agg(b):
                    i, r = nxt.tile(b), nxt.rows
                    pe.wait_ge(d_sc, ready(i))
                    pe.wait_ge(d_lo, reuse(i, 2))
                    for c in range(CHUNKS):
                        last = pe.transpose(ps[:, b % 2, c * P:c * P + r], scaled[0:r, b % 2, c * P:(c + 1) * P],
                                            ident[0:r, 0:r])
                    last.then_inc(d_t, 1)

                def project(b):
                    i, r = nxt.tile(b), nxt.rows
                    pe.wait_ge(d_lo, ready(i))
                    pe.wait_ge(d_h, reuse(i, 2))
                    split_mm(ps[0:r, 2 + b % 2, :], lambda a, c: aggt[:, b % 2, a, c, 0:r], lambda w, c: wnp[:, w, c, :],
                             CHUNKS).then_inc(d_mm, 1)

                def turn_x2(b):
                    i, r = cur.tile(b), cur.rows
                    pe.wait_ge(d_x2l, ready(i))
                    pe.wait_ge(d_xt, reuse(i, 2))
                    for k in range(2 * CHUNKS):
                        last = pe.transpose(bank16(4 + b % 2)[:, k * P:k * P + r], x2[0:r, b, k * P:(k + 1) * P],
                                            identh[0:r, 0:r])
                    last.then_inc(d_t2, 1)

                def gate(b):
                    i, r = cur.tile(b), cur.rows
                    pe.wait_ge(d_xt, ready(i))
                    at = (cur.par * HALF + b) * EXPERTS
                    split_mm(ps[0:r, 6, at:at + EXPERTS], lambda a, c: x2t[:, b % 2, a, c, 0:r],
                             lambda w, c: gwp[:, w, c, :], CHUNKS).then_inc(d_lg, 1)

                if nxt:
                    turn_agg(0)
                    for b in range(nxt.n):
                        if b + 1 < nxt.n:
                            turn_agg(b + 1)
                        project(b)
                if prev:
                    pe.wait_ge(d_mask, masks(prev.q, prev.n))
                    n, r = prev.n, prev.rows
                    pe.matmul(ps[0:r, 7, 0:n * EXPERTS], before16[0:r, 0:r], mask[0:r, 0:n, :].rearrange("p b e -> p (b e)"),
                              start=True, stop=False)
                    pe.matmul(ps[0:r, 7, 0:n * EXPERTS], ones16[:, 0:r], run[:, 0:n, :].rearrange("p b e -> p (b e)"),
                              start=False, stop=True).then_inc(d_pos, 1)
                if cur:
                    turn_x2(0)
                    for b in range(cur.n):
                        if b + 1 < cur.n:
                            turn_x2(b + 1)
                        gate(b)

            pipeline(pe, dense)

            pe.wait_ge(d_row, LAST + 1)
            pe.matmul(ps[0:EXPERTS, 6, 0:1], run[:, 0, :], ones16[:, 0:1], start=True, stop=True)
            pe.matmul(ps[0:1, 7, 0:EXPERTS], ones16[:, 0:1], run[:, 0, :], start=True, stop=True).then_inc(e_cnt, 1)
            pe.wait_ge(e_n, 1)
            pe.matmul(ps[0:EXPERTS + 1, 6, 1:2], before[0:EXPERTS, :], es[0:EXPERTS, 1:2], start=True, stop=True)
            pe.matmul(ps[0:EXPERTS + 1, 7, 0:1], shift[:, :], es[0:EXPERTS, 1:2], start=True, stop=True).then_inc(e_base, 1)
            pe.wait_ge(e_reach, 1)
            pe.matmul(ps[:, 0, 0:SLOTS], ones[0:EXPERTS + 1, :], reach[:, :], start=True, stop=True)
            pe.matmul(ps[0:1, 1, 0:SLOTS], es[0:EXPERTS + 1, 3:4], reach[:, :], start=True, stop=True).then_inc(e_list, 1)

            pe.wait_ge(e_w1, 16 * EXPERTS)
            pe.wait_ge(e_done, 1)

            def turn(it, b):
                k = RING * it + b
                pe.wait_ge(f_x[b], 16 * (it + 1))
                pe.wait_ge(f_xt, k + 1)
                for j in range(2 * CHUNKS):
                    last = pe.transpose(bank16(b)[:, j * P:(j + 1) * P], xf[:, b, j * P:(j + 1) * P], identh[:, :])
                last.then_inc(f_t, 1)

            def hidden(it, b):
                k = RING * it + b
                e = pe.value_load(expk[0:1, ds(k, 1)], min_val=0, max_val=EXPERTS - 1)
                pe.wait_ge(f_xt, RING + k + 1)
                pe.wait_ge(f_hid, k + 1)
                split_mm(ps[:, 3 + b, 0:FF].unsqueeze(1), lambda a, c: xft[:, b, a, c, :], lambda w, c: w1[:, ds(e, 1), c, w, :],
                         CHUNKS).then_inc(f_mm, 1)

            def collect(it, b):
                k = RING * it + b
                pe.wait_ge(f_hid, RING + k + 1)
                pe.wait_ge(f_hot, k + 1)
                pe.matmul(ps[0:EXPERTS, 6, 0:FF], hotk[:, b, :], hid[:, b, :], start=False, stop=False,
                          skip_group_check=True).then_inc(f_acc, 1)

            pe.matmul(ps[0:EXPERTS, 6, 0:FF], zero[:, 0:EXPERTS], zero[:, 0:FF], start=True, stop=False, skip_group_check=True)
            with pe.Fori(0, SLOTS // RING) as it:
                for b in range(RING):
                    turn(it, b)
                    if b:
                        hidden(it, b - 1)
                    if b > 1:
                        collect(it, b - 2)
                hidden(it, RING - 1)
                collect(it, RING - 2)
                collect(it, RING - 1)
            pe.matmul(ps[0:EXPERTS, 6, 0:FF], zero[:, 0:EXPERTS], zero[:, 0:FF], start=False, stop=True,
                      skip_group_check=True).then_inc(f_end, 1)

            pe.wait_ge(g_mean, 1)
            for c in range(FF // P):
                last = pe.transpose(ps[:, 7, c * EXPERTS:(c + 1) * EXPERTS], mean[0:EXPERTS, c * P:(c + 1) * P],
                                    ident[0:EXPERTS, 0:EXPERTS])
            last.then_inc(g_tr, 1)
            pe.wait_ge(g_diag, 1)
            for e in range(EXPERTS):
                if e % 4 == 0:
                    pe.wait_ge(g_w2[e // 4], 16 * 4)
                for c in range(FF // P):
                    last = pe.matmul(ps[0:EXPERTS, 0, :], diag[:, c, e, :], w2[:, e, c, :],
                                     start=e == 0 and c == 0, stop=e == EXPERTS - 1 and c == FF // P - 1)
            last.then_inc(g_y, 1)
            pe.wait_ge(g_ys, 1)
            pe.matmul(ps[:, 5, :], rep[0:EXPERTS, :], y16[0:EXPERTS, :], start=True, stop=True).then_inc(g_rep, 1)
            pe.wait_ge(g_yst, 1)

            def mix(it, n, rows):
                def turn_weights(b):
                    i = UNROLL * it + b
                    pe.wait_ge(g_rts, reuse(i, 2))
                    pe.matmul(ps[:, 1 + b % 2, 0:rows].unsqueeze(1), stack[0:rows, ds(i, 1), :], identb[0:rows, 0:rows],
                              start=True, stop=True).then_inc(g_rt, 1)

                def combine(b):
                    i = UNROLL * it + b
                    pe.wait_ge(g_rts, ready(i))
                    pe.wait_ge(g_x, reuse(i, 2))
                    pe.matmul(ps[0:rows, 3 + b % 2, :], mixt[:, b % 2, 0:rows], ystack[:, :],
                              start=True, stop=True).then_inc(g_o, 1)

                turn_weights(0)
                for b in range(n):
                    if b + 1 < n:
                        turn_weights(b + 1)
                    combine(b)

            rounds(pe, mix)

        @block.vector
        def _(dve):
            for s in (d_lo, d_h, d_lk, d_x1, g_x):
                dve.sem_inc(s, CREDIT)
            dve.sem_inc(c_sum, 2)
            dve.sem_inc(c_r, 1)
            dve.sem_inc(c_s, 1)
            dve.sem_inc(v_max, 1)
            dve.sem_inc(v_lo, 1)
            dve.sem_inc(f_xt, RING)

            ln = Count(dve, v_link, 0)
            NJ = TILES - 1
            dve.wait_ge(s_edge, 16 * 6)
            dve.tensor_copy(srcf[:, :, :], srci[:, :, :])
            ln.link(dve.tensor_copy(dstf[:, :, :], dsti[:, :, :]))
            ln.link(dve.tensor_reduce(most[:, :], dstf[:, :, :], X, ALU.max))
            dve.wait_ge(s_const, 1)
            ln.link(dve.tensor_scalar(turn[:, :], iota_p[:, EDGE_CHUNKS - 1:EDGE_CHUNKS], float(EDGE_TILES), 1e6,
                                      ALU.is_ge, ALU.mult))
            ln.link(dve.tensor_tensor(most[:, EDGE_CHUNKS - 1:EDGE_CHUNKS], most[:, EDGE_CHUNKS - 1:EDGE_CHUNKS],
                                      turn[:, :], ALU.add))
            dve.tensor_tensor(passed[:, :, :], bounds[:, :].unsqueeze(1).to_broadcast([P, EDGE_CHUNKS, NJ]),
                              most[:, :].unsqueeze(2).to_broadcast([P, EDGE_CHUNKS, NJ]), ALU.is_gt).then_inc(b_cmp, 1)
            dve.wait_ge(b_cnt, 1)
            ln.link(dve.tensor_tensor(turn[0:NJ, :], ps[0:NJ, 6, 0:1], iota_p[0:NJ, 0:1], ALU.add))
            dve.tensor_scalar(later[0:NJ, :], kvals[0:NJ, :], turn[0:NJ, :], None, ALU.is_gt).then_inc(b_later, 1)
            dve.wait_ge(b_jb, 1)
            H = STEPS // 2
            jsplit = jall[:, :].rearrange("p (h k) -> p h k", h=2)
            ln.link(dve.tensor_copy(jsplit, ps[:, 0:2, 0:H]))
            dve.tensor_copy(jrow[0:1, 0:STEPS], jall[0:1, :])
            ln.link(dve.tensor_tensor(tall[:, :], kvals[:, :], jall[:, :], ALU.subtract))
            for c in range(EDGE_CHUNKS):
                if c >= 2:
                    dve.wait_ge(b_acc, c - 1)
                dve.tensor_scalar(hit[:, c % 2, :], tall[:, :], iota_p[:, c:c + 1], None, ALU.is_equal).then_inc(b_hit, 1)
            dve.wait_ge(b_acc, EDGE_CHUNKS)
            dve.memset(dstrel[:, STEPS:KW], 0.0)
            dve.tensor_copy(idx_all[:, 0:STEPS].rearrange("p (h k) -> p h k", h=2), ps[:, 2:4, 0:H])
            ln.link(dve.scalar_tensor_tensor(dstrel[:, 0:STEPS].rearrange("p (h k) -> p h k", h=2), jsplit, -float(P),
                                             ps[:, 4:6, 0:H], ALU.mult, ALU.add))
            dve.memset(agg[:, 0:DIRTY, :], 0.0).then_inc(b_done, 1)
            count = ln.n
            dve.wait_ge(s_const, 2)

            MAGIC = 0x5f3759df
            CHAIN = 12

            def rstd_chain(ln, cols):
                v, g, f = var[:, 0:cols], guess[:, 0:cols], fix[:, 0:cols]
                ln.link(dve.tensor_scalar(f.bitcast(i32), v.bitcast(i32), 1, None, ALU.logical_shift_right))
                ln.link(dve.tensor_scalar(g.bitcast(i32), f.bitcast(i32), -1.0, float(MAGIC), ALU.mult, ALU.add))
                for _ in range(3):
                    ln.link(dve.tensor_tensor(f, g, g, ALU.mult))
                    ln.link(dve.scalar_tensor_tensor(f, f, -0.5, v, ALU.mult, ALU.mult))
                    ln.link(dve.scalar_tensor_tensor(g, f, 1.5, g, ALU.add, ALU.mult))

            A_LINKS = 2 + 11 + 2

            def norm_a(it, n, rows):
                for part in halves(it, n, rows):
                    ln = Count(dve, v_link, count + part.q * A_LINKS)
                    r, c0 = slice(0, rows), part.par * HALF
                    for m in range(part.n):
                        b = c0 + m
                        dve.wait_ge(a_x[b], 16 * (it + 1))
                        last = dve.bn_stats(stats[r, m, :], xin[r, b, :])
                    ln.link(last)
                    dve.nop(nofuse=True)
                    for m in range(part.n):
                        last = dve.bn_aggr(mv[r, m, :], stats[r, m, :])
                    ln.link(last)
                    ln.link(dve.tensor_scalar(var[:, 0:HALF], mv[:, 0:HALF, 1], EPS, None, ALU.add))
                    rstd_chain(ln, HALF)
                    at = ds(part.q * HALF, part.n)
                    dve.tensor_copy(rstd[r, at], guess[r, 0:part.n])
                    ln.link(dve.scalar_tensor_tensor(nmr[r, at], mv[r, 0:part.n, 0], -1.0, guess[r, 0:part.n], ALU.mult, ALU.mult))
                    dve.wait_ge(a_norm, CREDIT + HALF * part.q - HALF)
                    dve.tensor_scalar(gs[r, 0, c0:c0 + part.n], guess[r, 0:part.n], SCALE, None, ALU.mult)
                    dve.tensor_scalar(gb[r, 0, c0:c0 + part.n], nmr[r, at], SCALE, None, ALU.mult).then_inc(a_stat, 1)
                    assert ln.n == A_LINKS, ln.n

            rounds(dve, norm_a)
            count += A_LINKS * (LAST + 1)

            def powers(ln, n, to, turns):
                dve.wait_ge(w_tr, turns)
                w = wpow[0:n, :]
                ln.link(dve.tensor_reduce(w[:, 0:1], ps[0:n, 6, 0:P], X, ALU.max))
                ln.link(dve.tensor_scalar(w[:, 0:1], w[:, 0:1], 1e-30, None, ALU.max))
                ln.link(dve.tensor_scalar(w[:, 1:2].bitcast(i32), w[:, 0:1].bitcast(i32), 0x7f800000, None, ALU.bitwise_and))
                ln.link(dve.reciprocal(w[:, 2:3], w[:, 1:2]))
                ln.link(dve.tensor_scalar(w[:, 2:3], w[:, 2:3], TOP, None, ALU.mult))
                ln.link(dve.tensor_scalar(w[:, 1:2], w[:, 1:2], 1.0 / (TOP * SCALE), None, ALU.mult))
                dve.tensor_scalar(w[:, 4:4 + n], ident[0:n, 0:n], w[:, 2:3], None, ALU.mult)
                dve.tensor_scalar(w[:, 4 + n:4 + 2 * n], ident[0:n, 0:n], w[:, 1:2], None, ALU.mult).then_inc(w_diag, 1)
                dve.wait_ge(w_bc, turns)
                dve.tensor_copy(wscale[:, to:to + n], ps[:, 6, 256:256 + n])
                dve.tensor_copy(wscale[:, 4 + to:4 + to + n], ps[:, 6, 256 + n:256 + 2 * n]).then_inc(w_scale, 1)

            ln = Count(dve, v_link, count)
            dve.wait_ge(v_st, 16)
            dve.wait_ge(c_ss, 16)
            dve.wait_ge(c_rs, 16)
            for b in range(UNROLL):
                dve.wait_ge(a_st[b], 16)
            flat = lambda a: a.rearrange("p c n -> p (c n)")
            dve.tensor_reduce(wmax[:, 0:1], flat(ws[:, :, :]), X, ALU.max, apply_absolute_value=True)
            dve.tensor_reduce(wmax[:, 1:2], flat(wn[:, :, :]), X, ALU.max, apply_absolute_value=True)
            dve.tensor_reduce(wmax[:, 2:3], flat(gw[:, :, :]), X, ALU.max, apply_absolute_value=True).then_inc(w_max, 1)
            powers(ln, 3, 0, 1)
            dve.tensor_scalar(minus_alpha[:, :], alphab[:, :], -1.0, None, ALU.mult)
            dve.wait_ge(w_hi, 1)
            for k, (raw, parts) in enumerate(((ws, wsp), (wn, wnp), (gw, gwp))):
                last = dve.scalar_tensor_tensor(parts[:, 1, :, :], raw[:, :, :], wscale[:, k:k + 1], parts[:, 0, :, :],
                                                ALU.mult, ALU.subtract)
            last.then_inc(w_lo, 1)
            count += ln.n

            dve.wait_ge(s_zero, 1)

            def one_hots(q, h):
                dve.wait_ge(c_step, SHALF * q + SHALF)
                dve.tensor_tensor(hot[:, h, :, :], iota_row[:, :].unsqueeze(1).to_broadcast([P, SHALF, P]),
                                  dstrel[:, ds(SHALF * q, SHALF)].unsqueeze(2).to_broadcast([P, SHALF, P]),
                                  ALU.is_equal).then_inc(c_hot, 1)

            def add_step(it, s):
                k = BODY * it + s
                j = dve.value_load(jrow[0:1, ds(k, 1)], min_val=0, max_val=TILES - 1)
                dve.wait_ge(c_step, BODY + k + 1)
                dve.wait_ge(c_sum, 2 + k)
                r = 2 * (s % 2)
                dve.tensor_tensor(agg[:, ds(j, 1), :], agg[:, ds(j, 1), :],
                                  ps[:, r:r + 2, :].rearrange("p a n -> p (a n)")[:, 0:D + 1].unsqueeze(1),
                                  ALU.add).then_inc(c_sum, 1)

            def side(it, rows, w1_turn, s):
                if w1_turn == "max" and s == 6:
                    dve.wait_ge(v_ld, 16 * (it + 1))
                    dve.tensor_reduce(wmax[:, ds(it + 3, 1)], flat(stage[:, :, :]), X, ALU.max,
                                      apply_absolute_value=True).then_inc(v_max, 1)
                if w1_turn == "split" and s == 6:
                    dve.wait_ge(v_hi, it - EXPERTS + 1)
                    dve.scalar_tensor_tensor(staged[:, :, 1, :], stage[:, :, :], wscale[:, 3:4], staged[:, :, 0, :],
                                             ALU.mult, ALU.subtract).then_inc(v_lo, 1)
                i = it
                if rows and s == 4:
                    dve.wait_ge(c_xn, i + 1)
                    dve.wait_ge(c_rs, 16 * (i + 1))
                    dve.tensor_tensor(cr[0:rows, :], cx[0:rows, :], cxn[0:rows, :], ALU.add).then_inc(c_r, 1)
                if rows and s == 13:
                    dve.wait_ge(c_mm, i + 2)
                    dve.wait_ge(c_ss, 16 * (i + 1))
                    dve.scalar_tensor_tensor(cs[0:rows, :], ps[0:rows, 5, :], wscale[0:rows, 4:5], bself[0:rows, :],
                                             ALU.mult, ALU.add).then_inc(c_s, 1)

            def body(it, rows, w1_turn):
                one_hots(2 * it + 1, 1)
                for s in range(BODY):
                    add_step(it, s)
                    if s == SHALF - 1:
                        one_hots(2 * it + 2, 0)
                    side(it, rows, w1_turn, s)

            one_hots(0, 0)
            with dve.Fori(0, EXPERTS) as it:
                body(it, P, "max")
            ln = Count(dve, v_link, count)
            dve.wait_ge(v_max, EXPERTS + 1)
            dve.tensor_reduce(wmax[:, 2:3], wmax[:, 3:3 + EXPERTS], X, ALU.max).then_inc(w_max, 1)
            powers(ln, 1, 3, 2)
            count += ln.n
            with dve.Fori(EXPERTS, 2 * EXPERTS) as it:
                body(it, P, "split")
            with dve.Fori(2 * EXPERTS, TILES - 1) as it:
                body(it, P, None)
            body(TILES - 1, TAIL, None)
            with dve.Fori(TILES, STEP_ROUNDS) as it:
                body(it, 0, None)

            dve.wait_ge(c_sum, 2 + STEPS)
            dve.wait_ge(c_ss, 16 * (TILES + 1))
            dve.wait_ge(c_rs, 16 * (TILES + 1))
            dve.wait_ge(v_st, 16 * (EXPERTS + 1))
            ln = Count(dve, v_link, count)
            ln.link(dve.memset(run[:, 0, :], 0.0))
            ln.link(dve.tensor_scalar(inv[:, :], agg[:, :, D], 1.0, None, ALU.max))
            dve.reciprocal(inv[:, :], inv[:, :]).then_inc(d_inv, 1)
            count += ln.n
            CHAIN_LINKS, ROUTE_LINKS = 15, 17

            def dense(nxt, cur, prev):
                def low(b):
                    i, r = nxt.tile(b), nxt.rows
                    dve.wait_ge(d_hi, ready(i))
                    dve.tensor_tensor(aggt[:, b % 2, 1, :, 0:r],
                                      ps[:, b % 2, :].rearrange("p (c n) -> p c n", c=CHUNKS)[:, :, 0:r],
                                      aggt[:, b % 2, 0, :, 0:r], ALU.subtract).then_inc(d_lo, 1)

                def add_self(b):
                    i, r = nxt.tile(b), slice(0, nxt.rows)
                    dve.wait_ge(d_mm, ready(i))
                    dve.wait_ge(d_s[b % 2], 16 * (2 * nxt.q + b // 2 + 1))
                    dve.scalar_tensor_tensor(agg[r, ds(i, 1), 0:D], ps[r, 2 + b % 2, :].unsqueeze(1), wscale[r, 5:6],
                                             sbuf[r, b % 2, :].unsqueeze(1), ALU.mult, ALU.add).then_inc(d_h, 1)

                def stats_h(b):
                    i, r = nxt.tile(b), slice(0, nxt.rows)
                    dve.wait_ge(d_h, ready(i))
                    dve.nop(nofuse=True)
                    return dve.bn_stats(stats[r, b, :], agg[r, ds(i, 1), 0:D])

                def add_residual(b):
                    i, r = cur.tile(b), slice(0, cur.rows)
                    slot = agg[r, ds(i, 1), 0:D]
                    dve.wait_ge(d_pr, ready(i))
                    dve.wait_ge(d_r[b % 2], 16 * (2 * cur.q + b // 2 + 1))
                    part = rbuf[r, b % 2, :]
                    dve.scalar_tensor_tensor(part, below[r, b % 2, :], minus_alpha[r, :], part, ALU.mult, ALU.add).then_inc(d_lk, 1)
                    dve.wait_ge(d_lk, ready(i))
                    dve.scalar_tensor_tensor(slot, slot, 0.0, part.unsqueeze(1), ALU.max, ALU.add).then_inc(d_x1, 1)

                def stats_x1(b):
                    i, r = cur.tile(b), slice(0, cur.rows)
                    dve.wait_ge(d_x1, ready(i))
                    dve.nop(nofuse=True)
                    return dve.bn_stats(stats[r, HALF + b, :], agg[r, ds(i, 1), 0:D])

                for b in range(HALF):
                    if nxt and b < nxt.n:
                        low(b)
                    if cur and b < cur.n:
                        add_residual(b)
                    if nxt and 0 < b <= nxt.n - 1:
                        add_self(b - 1)
                    if cur and b < cur.n:
                        last = stats_x1(b)
                    if nxt and 0 < b <= nxt.n - 1:
                        last = stats_h(b - 1)
                if nxt:
                    add_self(nxt.n - 1)
                    last = stats_h(nxt.n - 1)
                if nxt or cur:
                    turn_no = nxt.q if nxt else cur.q + 1
                    par = nxt.par if nxt else 1 - cur.par
                    ln = Count(dve, k_link, turn_no * CHAIN_LINKS)
                    ln.link(last)
                    dve.nop(nofuse=True)
                    for on, at in ((nxt, 0), (cur, HALF)):
                        if on:
                            for b in range(on.n):
                                last = dve.bn_aggr(mv[0:on.rows, UNROLL + at + b, :], stats[0:on.rows, at + b, :])
                    ln.link(last)
                    mean_var = mv[:, UNROLL:2 * UNROLL, :]
                    ln.link(dve.tensor_scalar(var[:, :], mean_var[:, :, 1], EPS, None, ALU.add))
                    rstd_chain(ln, UNROLL)
                    dve.tensor_copy(gs[:, par, 0:HALF], guess[:, 0:HALF])
                    ln.link(dve.tensor_scalar(gs[:, par, HALF:UNROLL], guess[:, HALF:UNROLL], SCALE, None, ALU.mult))
                    dve.scalar_tensor_tensor(gb[:, par, :], mean_var[:, :, 0], -1.0, gs[:, par, :], ALU.mult,
                                             ALU.mult).then_inc(d_stat, 1)
                    assert ln.n == CHAIN_LINKS, ln.n
                if not prev:
                    return
                n, rows = prev.n, prev.rows
                r, m = slice(0, rows), slice(0, n)
                ln = Count(dve, r_link, prev.q * ROUTE_LINKS)
                dve.wait_ge(d_lg, ready(prev.tile(n - 1)))
                at = ds(prev.q * HALF, n)
                wide = lambda a: a.unsqueeze(2).to_broadcast([rows, n, EXPERTS])
                over = lambda a: a[r, :].unsqueeze(1).to_broadcast([rows, n, EXPERTS])
                col = prev.par * HALF * EXPERTS
                ln.link(dve.tensor_copy(logit[r, m, :], ps[r, 6, col:col + n * EXPERTS].rearrange("p (b e) -> p b e", b=n)))
                for k, (vals, pickd) in enumerate(((logit, first), (logit2, second))):
                    best = top[r, k, at]
                    ln.link(dve.tensor_reduce(best, vals[r, m, :], X, ALU.max))
                    ln.link(dve.tensor_tensor(cand[r, m, :], vals[r, m, :], wide(best), ALU.is_equal))
                    ln.link(dve.tensor_tensor(cand[r, m, :], cand[r, m, :], over(pick), ALU.mult))
                    ln.link(dve.tensor_reduce(lead[r, m], cand[r, m, :], X, ALU.max))
                    ln.link(dve.tensor_tensor(pickd[r, at, :], cand[r, m, :], wide(lead[r, m]), ALU.is_equal))
                    if k == 0:
                        ln.link(dve.scalar_tensor_tensor(logit2[r, m, :], first[r, at, :], -3.0e38, logit[r, m, :],
                                                         ALU.mult, ALU.add))
                counted = dve.tensor_tensor(mask[r, m, :], first[r, at, :], second[r, at, :], ALU.add)
                for b in range(n - 1):
                    counted.then_inc(d_mask, 1)
                    dve.wait_ge(d_mask, masks(prev.q, b + 1))
                    counted = dve.tensor_tensor(run[r, b + 1, :], run[r, b, :], mask[r, b, :], ALU.add)
                counted.then_inc(d_mask, 1)
                dve.wait_ge(d_mask, masks(prev.q, n))
                dve.wait_ge(d_pos, prev.q + 1)
                dve.tensor_tensor(spot[r, m, :], ps[r, 7, 0:n * EXPERTS].rearrange("p (b e) -> p b e", b=n),
                                  over(ecap), ALU.add)
                ln.link(dve.tensor_tensor(run[r, 0, :], run[r, n - 1, :], mask[r, n - 1, :], ALU.add))
                for k, pickd in enumerate((first, second)):
                    ln.link(dve.tensor_tensor(prod[r, m, :], pickd[r, at, :], spot[r, m, :], ALU.mult))
                    ln.link(dve.tensor_reduce(rowf[r, k, m], prod[r, m, :], X, ALU.add))
                for b in range(HALF):
                    dve.wait_ge(d_sc1[b], 16 * (prev.q + 1))
                    dve.wait_ge(d_sc2[b], 16 * (prev.q + 1))
                dve.tensor_copy(row[r, prev.par, :, m], rowf[r, :, m]).then_inc(d_row, 1)
                assert ln.n == ROUTE_LINKS, ln.n

            pipeline(dve, dense)

            ln = Count(dve, v_link, count)
            E1 = EXPERTS + 1
            dve.wait_ge(e_cnt, 1)
            ln.link(dve.tensor_copy(es[0:EXPERTS, 0:1], ps[0:EXPERTS, 6, 0:1]))
            ln.link(dve.tensor_tensor(fillrow[0:1, :], ps[0:1, 7, 0:EXPERTS], ecap[0:1, :], ALU.add))
            ln.link(dve.tensor_scalar(steps49[:, :], steps49[:, :], es[0:EXPERTS, 0:1], None, ALU.is_lt))
            dve.tensor_reduce(es[0:EXPERTS, 1:2], steps49[:, :], X, ALU.add).then_inc(e_n, 1)
            dve.tensor_tensor(top[:, 1, :], top[:, 1, :], top[:, 0, :], ALU.subtract).then_inc(g_ex, 1)
            ln.link(dve.tensor_scalar(es[0:EXPERTS, 4:5], es[0:EXPERTS, 0:1], 1.0, None, ALU.max))
            dve.reciprocal(es[0:EXPERTS, 5:6], es[0:EXPERTS, 4:5])
            dve.wait_ge(e_base, 1)
            dve.tensor_copy(es[0:E1, 2:3], ps[0:E1, 6, 1:2])
            ln.link(dve.tensor_scalar(es[0:E1, 3:4], ps[0:E1, 7, 0:1], -float(P), float(CAP), ALU.mult, ALU.add))
            dve.tensor_scalar(reach[:, :], iota_row[0:E1, 0:SLOTS], es[0:E1, 2:3], None, ALU.is_ge).then_inc(e_reach, 1)
            dve.wait_ge(e_list, 1)
            past = erow[:, 0, :]
            ln.link(dve.tensor_copy(past, ps[:, 0, 0:SLOTS]))
            one, two, three = erow[0:1, 1, :], erow[0:1, 2, :], erow[0:1, 3, :]
            dve.tensor_scalar(expk[0:1, :], past[0:1, :], float(EXPERTS), -1.0, ALU.min, ALU.add)
            dve.tensor_scalar(two, past[0:1, :], float(EXPERTS), None, ALU.is_gt)
            ln.link(dve.scalar_tensor_tensor(one, iota_row[0:1, 0:SLOTS], float(P), ps[0:1, 1, 0:SLOTS], ALU.mult, ALU.add))
            dve.tensor_scalar(one, one, -float(CAP), None, ALU.add)
            ln.link(dve.tensor_scalar(three, two, -1.0, 1.0, ALU.mult, ALU.add))
            ln.link(dve.tensor_tensor(one, one, three, ALU.mult))
            dve.scalar_tensor_tensor(rowk[0:1, :], two, float(DUMMY), one, ALU.mult, ALU.add)
            for b in range(HALF):
                dve.wait_ge(d_sc1[b], 16 * (1 + LAST + (b == 0)))
                dve.wait_ge(d_sc2[b], 16 * (1 + LAST + (b == 0)))
            dve.tensor_tensor(hote[:, :, :], past.unsqueeze(2).to_broadcast([P, SLOTS, EXPERTS]),
                              iota_row[:, 1:EXPERTS + 1].unsqueeze(1).to_broadcast([P, SLOTS, EXPERTS]),
                              ALU.is_equal).then_inc(e_done, 1)
            dve.wait_ge(g_exd, 1)
            ln.link(dve.tensor_scalar(top[:, 0, :], top[:, 1, :], 1.0, None, ALU.add))
            ln.link(dve.reciprocal(top[:, 0, :], top[:, 0, :]))
            dve.tensor_tensor(top[:, 1, :], top[:, 1, :], top[:, 0, :], ALU.mult).then_inc(g_soft, 1)
            count += ln.n

            dve.wait_ge(e_done, 1)
            with dve.Fori(0, SLOTS // RING) as it:
                for b in range(RING):
                    k = RING * it + b
                    dve.wait_ge(f_acc, k + 1)
                    dve.tensor_copy(hotk[:, b:b + 1, :], hote[:, ds(k, 1), :]).then_inc(f_hot, 1)
                    dve.wait_ge(f_t, RING + k + 1)
                    dve.wait_ge(f_mm, k + 1)
                    dve.tensor_copy(xft[:, b, :, :, :], chunks16(bank16(b), P)).then_inc(f_xt, 1)

            ln = Count(dve, v_link, count)
            dve.wait_ge(f_end, 1)
            dve.wait_ge(g_mixw, 1)
            dve.tensor_scalar(mean[0:EXPERTS, 0:FF], ps[0:EXPERTS, 6, 0:FF], es[0:EXPERTS, 5:6], None,
                              ALU.mult).then_inc(g_mean, 1)
            part = lambda k: stack[:, :, k * EXPERTS:(k + 1) * EXPERTS]
            w = mixw[:, 0, :, :]
            for k, copies in ((0, (2, 4)), (1, (3, 5)), (6, (7,))):
                ln.link(dve.tensor_copy(part(k), w))
                for c in copies:
                    last = dve.tensor_copy(part(c), part(k))
                if k != 6:
                    ln.link(dve.tensor_tensor(w, w, part(k), ALU.subtract))
            dve.tensor_copy(rep[0:EXPERTS, :].rearrange("p (a e) -> p a e", a=8),
                            ident[0:EXPERTS, 0:EXPERTS].unsqueeze(1).to_broadcast([EXPERTS, 8, EXPERTS]))
            ln.link(dve.tensor_tensor(same, pick[:, :].unsqueeze(2).to_broadcast([P, EXPERTS, EXPERTS]),
                                      pick[:, :].unsqueeze(1).to_broadcast([P, EXPERTS, EXPERTS]), ALU.is_equal))
            dve.wait_ge(g_trs, 1)
            for c in range(FF // P):
                last = dve.tensor_tensor(diag[:, c, :, :], same,
                                         es2[:, c * EXPERTS:(c + 1) * EXPERTS].unsqueeze(2).to_broadcast([P, EXPERTS, EXPERTS]),
                                         ALU.mult)
            last.then_inc(g_diag, 1)
            dve.wait_ge(g_y, 1)
            dve.tensor_copy(y16[0:EXPERTS, :], ps[0:EXPERTS, 0, :]).then_inc(g_ys, 1)
            dve.wait_ge(g_rep, 1)
            yr = ps[:, 5, :]
            ln.link(dve.tensor_copy(yp[:, 0, :], yr))
            ln.link(dve.tensor_tensor(ylow, yr, yp[:, 0, :], ALU.subtract))
            ln.link(dve.tensor_copy(yp[:, 1, :], ylow))
            dve.tensor_scalar(es[:, 6:7], iota_p[:, 0:1], float(7 * EXPERTS), None, ALU.is_ge)
            ln.link(dve.tensor_tensor(ylow, ylow, yp[:, 1, :], ALU.subtract))
            dve.tensor_copy(ystack[0:32, :], yp[0:32, 0, :])
            dve.tensor_copy(ystack[32:64, :], yp[32:64, 1, :])
            dve.tensor_copy(ystack[64:96, :], ylow[64:96, :])
            ln.link(dve.tensor_scalar(ylow[96:128, :], yp[96:128, 1, :], es[96:128, 6:7], None, ALU.mult))
            ln.link(dve.tensor_scalar(es[:, 7:8], es[:, 6:7], -1.0, 1.0, ALU.mult, ALU.add))
            dve.scalar_tensor_tensor(ystack[96:128, :], yp[96:128, 0, :], es[96:128, 7:8], ylow[96:128, :], ALU.mult,
                                     ALU.add).then_inc(g_yst, 1)
            count += ln.n

            def mix(it, n, rows):
                for b in range(n):
                    i = UNROLL * it + b
                    slot = agg[0:rows, ds(i, 1), 0:D]
                    dve.wait_ge(g_o, ready(i))
                    dve.tensor_tensor(slot, slot, ps[0:rows, 3 + b % 2, :].unsqueeze(1), ALU.add).then_inc(g_x, 1)

            rounds(dve, mix)


def kernel(x, src, dst, L0_gnn_W_self, L0_gnn_b_self, L0_gnn_W_neigh, L0_gnn_gamma, L0_gnn_beta, L0_gnn_alpha,
           L0_ffn_gate_weight, L0_ffn_w1, L0_ffn_w2):
    import numpy as np
    import concourse.bacc as bacc
    from concourse.bass_utils import run_bass_kernel_spmd

    arrays = {
        "x": x, "src": src, "dst": dst,
        "w_self": L0_gnn_W_self, "b_self": np.asarray(L0_gnn_b_self).reshape(1, D), "w_neigh": L0_gnn_W_neigh,
        "gamma": np.asarray(L0_gnn_gamma).reshape(1, D), "beta": np.asarray(L0_gnn_beta).reshape(1, D),
        "alpha": np.asarray(L0_gnn_alpha).reshape(1, 1),
        "gate_t": np.asarray(L0_ffn_gate_weight).T,
        "w1_t": np.asarray(L0_ffn_w1).reshape(EXPERTS * FF, D).T,
        "w2_t": np.asarray(L0_ffn_w2).transpose(0, 2, 1),
    }
    arrays = {f"in_{n}": np.ascontiguousarray(a) for n, a in arrays.items()}
    nc = bacc.Bacc("TRN2", target_bir_lowering=False, num_devices=1)
    args = [nc.dram_tensor(n, a.shape, mybir.dt.from_np(a.dtype), kind="ExternalInput").ap() for n, a in arrays.items()]
    args.append(nc.dram_tensor("out_x", (N, D), mybir.dt.float32, kind="ExternalOutput").ap())
    build(nc, *args)
    r = run_bass_kernel_spmd(nc, [arrays], core_ids=[0])
    return r.results[0]["out_x"]
```
